# Optimizing a Trainium2 kernel written in Bass

```python
import numpy as np
import jax
import jax.numpy as jnp

def _softmax(x, axis=-1):
    return jax.nn.softmax(x, axis=axis)

def _gelu(x):
    return jax.nn.gelu(x, approximate=True)

def _silu(x):
    return jax.nn.silu(x)

def _sigmoid(x):
    return jax.nn.sigmoid(x)

def _layernorm(x, axis=-1, eps=1e-05):
    m = jnp.mean(x, axis=axis, keepdims=True)
    v = jnp.var(x, axis=axis, keepdims=True)
    return (x - m) / jnp.sqrt(v + eps)

def _scatter_add(tgt, idx, src, axis=0):
    return tgt.at[idx].add(src)

def _segment_sum(src, seg, n):
    return jax.ops.segment_sum(src, seg, n)
kernel_name = 'mk_recurrent_d1_jaxref_r8_7a787b'

def setup_inputs(seed: int=0):
    np.random.seed(seed)
    _w = jnp.asarray

    def _L0_attn_setup():
        import jax, jax.numpy as jnp
        import numpy as np
        NUM_HEADS = 1
        LN_EPS = 1e-05
        key = jax.random.key(seed)
        ks = jax.random.split(key, 4)
        B, L, D = (8, 512, 128)
        x = jax.random.normal(ks[0], (B, L, D), dtype=jnp.float32)
        qkv_w = jax.random.normal(ks[1], (3 * D, D), dtype=jnp.float32) * np.float32(np.sqrt(1.0 / D))
        qkv_b = jnp.zeros((3 * D,), dtype=jnp.float32)
        proj_w = jax.random.normal(ks[2], (D, D), dtype=jnp.float32) * np.float32(np.sqrt(1.0 / D))
        proj_b = jnp.zeros((D,), dtype=jnp.float32)
        return {'x': x, 'norm_w': jnp.ones((D,), dtype=jnp.float32), 'norm_b': jnp.zeros((D,), dtype=jnp.float32), 'qkv_w': qkv_w, 'qkv_b': qkv_b, 'proj_w': proj_w, 'proj_b': proj_b}
    _L0_attn_in = _L0_attn_setup()

    def _L0_ffn_setup():
        import jax, jax.numpy as jnp
        import numpy as np
        TOP_K = 8
        key = jax.random.key(seed)
        ks = jax.random.split(key, 5)
        B, S, H = (2, 256, 128)
        E, F = (16, 352)
        return {'hidden_states': jax.random.normal(ks[0], (B, S, H), dtype=jnp.float32), 'router_w': jax.random.normal(ks[1], (E, H), dtype=jnp.float32) * (1.0 / np.sqrt(H)), 'gate_w': jax.random.normal(ks[2], (E, F, H), dtype=jnp.float32) * (1.0 / np.sqrt(H)), 'up_w': jax.random.normal(ks[3], (E, F, H), dtype=jnp.float32) * (1.0 / np.sqrt(H)), 'down_w': jax.random.normal(ks[4], (E, H, F), dtype=jnp.float32) * (1.0 / np.sqrt(F))}
    _L0_ffn_in = _L0_ffn_setup()
    _d = {'L0_attn_x': _L0_attn_in['x'], 'L0_attn_norm_w': _L0_attn_in['norm_w'], 'L0_attn_norm_b': _L0_attn_in['norm_b'], 'L0_attn_qkv_w': _L0_attn_in['qkv_w'], 'L0_attn_qkv_b': _L0_attn_in['qkv_b'], 'L0_attn_proj_w': _L0_attn_in['proj_w'], 'L0_attn_proj_b': _L0_attn_in['proj_b'], 'L0_ffn_router_w': _L0_ffn_in['router_w'], 'L0_ffn_gate_w': _L0_ffn_in['gate_w'], 'L0_ffn_up_w': _L0_ffn_in['up_w'], 'L0_ffn_down_w': _L0_ffn_in['down_w']}
    _x0 = _d['L0_attn_x']
    _d['L0_attn_x'] = jax.random.normal(jax.random.fold_in(jax.random.key(seed), 1), (4, 512, 128), dtype=_x0.dtype)
    del _x0
    return _d

def reference(L0_attn_x, L0_attn_norm_w, L0_attn_norm_b, L0_attn_qkv_w, L0_attn_qkv_b, L0_attn_proj_w, L0_attn_proj_b, L0_ffn_router_w, L0_ffn_gate_w, L0_ffn_up_w, L0_ffn_down_w):

    def _L0_attn_ref(x, norm_w, norm_b, qkv_w, qkv_b, proj_w, proj_b):
        import jax, jax.numpy as jnp
        import numpy as np
        NUM_HEADS = 1
        LN_EPS = 1e-05
        B, L, D = x.shape
        H = NUM_HEADS
        mu = jnp.mean(x, axis=-1, keepdims=True)
        var = jnp.mean(jnp.square(x - mu), axis=-1, keepdims=True)
        h = (x - mu) / jnp.sqrt(var + LN_EPS) * norm_w + norm_b
        qkv = h @ qkv_w.T + qkv_b
        qkv = qkv.reshape(B * H, L // H, 3, D)
        q, k, v = (qkv[..., 0, :], qkv[..., 1, :], qkv[..., 2, :])
        scale = np.float32(1.0 / np.sqrt(L // H))
        w = jax.nn.softmax(jnp.einsum('ncq,nck->nqk', q, k * scale), axis=2)
        a = jnp.einsum('nqk,nck->ncq', w, v)
        a = a.reshape(B, L, D)
        return a @ proj_w.T + proj_b + x

    def _L0_ffn_ref(hidden_states, router_w, gate_w, up_w, down_w):
        import jax, jax.numpy as jnp
        import numpy as np
        TOP_K = 8
        B, S, H = hidden_states.shape
        E = router_w.shape[0]
        x = hidden_states.reshape(-1, H)
        T = x.shape[0]
        logits = x @ router_w.T
        topk_vals, topk_idx = jax.lax.top_k(logits, TOP_K)
        topk_w = jax.nn.softmax(topk_vals, axis=-1)
        dense_w = jnp.zeros((T, E), dtype=x.dtype).at[jnp.arange(T)[:, None], topk_idx].add(topk_w)
        g = jnp.einsum('th,efh->etf', x, gate_w)
        u = jnp.einsum('th,efh->etf', x, up_w)
        h = jax.nn.silu(g) * u
        out_e = jnp.einsum('etf,ehf->eth', h, down_w)
        out = jnp.einsum('te,eth->th', dense_w, out_e)
        return out.reshape(B, S, H)
    x = L0_attn_x
    xn = _layernorm(x, axis=-1)
    s = _L0_attn_ref(xn, L0_attn_norm_w, L0_attn_norm_b, L0_attn_qkv_w, L0_attn_qkv_b, L0_attn_proj_w, L0_attn_proj_b)
    g = _silu(_L0_ffn_ref(xn, L0_ffn_router_w, L0_ffn_gate_w, L0_ffn_up_w, L0_ffn_down_w))
    x = x + s * g
    return x

_drawn_inputs = setup_inputs


def setup_inputs(seed=0):
    import zlib

    import numpy as np

    out = dict(_drawn_inputs(seed))
    spreads = {'L0_attn_norm_w': (1.0, 0.2),
     'L0_attn_norm_b': (0.0, 0.393),
     'L0_attn_qkv_b': (0.0, 0.351),
     'L0_attn_proj_b': (0.0, 0.561)}
    factors = {}
    for name, (base, spread) in spreads.items():
        noise = np.random.default_rng([zlib.crc32(name.encode()), seed]).standard_normal(out[name].shape)
        drawn = base * np.exp(spread * noise) if base else spread * noise
        out[name] = jnp.asarray(drawn.astype(out[name].dtype))
    for name, factor in factors.items():
        out[name] = (out[name] * factor).astype(out[name].dtype)
    return out
```

```python
from contextlib import ExitStack

import concourse.bass as bass
from concourse import mybir

F32 = mybir.dt.float32
F32R = mybir.dt.float32r
ALU = mybir.AluOpType
ACT = mybir.ActivationFunctionType
AX_X = mybir.AxisListType.X

P = 128
LN_EPS = 1e-5
TOP_K = 8
LAG = 3
RING = 3
CHUNK = 2
STAGES = 2
AHEAD = 4
NEG = -3.4028235e38


def block_pattern(n, per_expert):
    out, f = [], n * P
    while f < (n + 1) * P:
        e = f // per_expert
        end = min((e + 1) * per_expert, (n + 1) * P)
        out.append((e, f - n * P, end - n * P))
        f = end
    return out


def gated_block(nc, x, norm_w, norm_b, wqkvT, wv, qkv_b, projT, proj_b, routerT, w_all, dense_dram, out):
    B, L, D = x.shape
    E = routerT.shape[1]
    NB = w_all.shape[1]
    FE = NB * P // E
    CH = L // P
    NCHUNK = NB // CHUNK
    SCALE = float(L) ** -0.5
    assert D == P and L == 512 and NB % CHUNK == 0 and E * CH <= P

    patterns, pattern_of = [], []
    for n in range(NB):
        cut = block_pattern(n, FE)
        if not patterns or patterns[-1] != cut:
            patterns.append(cut)
        pattern_of.append(len(patterns) - 1)
    last_block = [max(n for n in range(NB) if pattern_of[n] == q) for q in range(len(patterns))]
    SLOTS = 7
    assert len(patterns) % SLOTS == 0
    ROUNDS = len(patterns) // SLOTS
    slot_step = [16 * len(patterns[s]) for s in range(SLOTS)]
    assert all(16 * len(c) == slot_step[q % SLOTS] for q, c in enumerate(patterns))

    def prev(n, depth):
        if n >= depth:
            return 0, n - depth
        return -1, max(m for m in range(NB) if m % depth == n % depth)

    with ExitStack() as ctx:
        def sb(name, shape, dt=F32):
            return ctx.enter_context(nc.sbuf_tensor(name, shape, dt))

        def sem(name):
            return ctx.enter_context(nc.semaphore(name))

        psum = ctx.enter_context(nc.psum_tensor("psum", [P, 8, 512], F32))
        gate_ps = [psum[:, r, :] for r in range(RING)]
        up_ps = [psum[:, RING + r, :] for r in range(RING)]
        ffn_ps = psum[:, 6, :]
        misc = psum[:, 7, :]

        w_hi = sb("w_hi", [P, NB, 3, P], F32R)
        w_lo = sb("w_lo", [P, NB, 3, P], F32R)
        xT_hi = sb("xT_hi", [P, B * L], F32R)
        xT_lo = sb("xT_lo", [P, B * L], F32R)
        xn = sb("xn", [P, B * CH, D])
        route = sb("route", [P, SLOTS, L])
        s_buf = sb("s_buf", [P, RING, L])
        h_hi = sb("h_hi", [P, RING, L], F32R)
        h_lo = sb("h_lo", [P, RING, L], F32R)
        stage = sb("stage", [P, STAGES, CHUNK * 3 * P])
        tail = stage[:, :, :].rearrange("p s n -> p (s n)")
        yT = tail[:, 0:L]
        o_sb = tail[:, L:2 * L].rearrange("p (j d) -> p j d", j=CH)
        x_again = tail[:, 2 * L:3 * L].rearrange("p (j d) -> p j d", j=CH)

        wqkv_raw = sb("wqkv_raw", [P, 3 * D])
        wqkT = sb("wqkT", [P, 2 * D])
        wv_n = sb("wv_n", [P, D])
        proj_sb = sb("proj_sb", [P, D])
        nb_bc = sb("nb_bc", [P, P])
        nw_bc = sb("nw_bc", [P, D])
        bk_bc = sb("bk_bc", [P, D])
        bv_bc = sb("bv_bc", [P, P])
        pb_bc = sb("pb_bc", [P, D])
        ident = sb("ident", [P, P])
        bqk_row = sb("bqk_row", [1, 2 * D])
        bkL_row = sb("bkL_row", [1, D])
        r_row = sb("r_row", [1, D])
        rt_raw = sb("rt_raw", [P, E])
        rt_hi = sb("rt_hi", [P, E], F32R)
        rt_lo = sb("rt_lo", [P, E], F32R)
        cols = sb("cols", [P, 3])
        stats = sb("stats", [P, CH, 6])
        mv = sb("mv", [P, CH, 2])
        ve = sb("ve", [P, 2 * CH])
        mhalf = sb("mhalf", [P, CH])
        rstd = sb("rstd", [P, CH])
        r2 = sb("r2", [P, B * CH])
        r2_cur = sb("r2_cur", [P, CH])
        sm = sb("sm", [P, 4])
        rsum = sb("rsum", [P, 2 * 3 * CH])

        scratch = sb("scratch", [P, 4 * 129 + 2 * 130 + P])
        z = scratch[:, 0:CH * 129].rearrange("p (j d) -> p j d", j=CH)
        x_cur = scratch[:, 0:L]
        mat_a = scratch[:, 516:516 + 129]
        mat_b = scratch[:, 646:646 + D]
        out_bias = scratch[:, 776:776 + D]
        NR = 3 * CH
        lg = scratch[:, 0:NR * E].rearrange("p (j e) -> p j e", e=E)
        lr = scratch[:, NR * E:2 * NR * E].rearrange("p (j e) -> p j e", e=E)
        ex = scratch[:, 2 * NR * E:3 * NR * E].rearrange("p (j e) -> p j e", e=E)
        dense = scratch[:, 3 * NR * E:4 * NR * E].rearrange("p (b e j) -> p b e j", e=E, j=CH)
        top8 = scratch[:, 4 * NR * E:4 * NR * E + NR * 8].rearrange("p (j k) -> p j k", k=8)
        denseT = scratch[0:E * CH, 0:3 * P]

        s_x = [sem(f"s_x{b}") for b in range(B)]
        s_const = sem("s_const")
        s_rtc = sem("s_rtc")
        s_wload = [sem(f"s_wload{i}") for i in range(STAGES)]
        s_whi, s_wlo = sem("s_whi"), sem("s_wlo")
        s_route = [sem(f"s_route{i}") for i in range(SLOTS)]
        s_xagain, s_out = sem("s_xagain"), sem("s_out")
        s_ident = sem("s_ident")
        s_dve = sem("s_dve")
        s_pool = sem("s_pool")
        s_var, s_rstd, s_ln, s_r2 = sem("s_var"), sem("s_rstd"), sem("s_ln"), sem("s_r2")
        s_xpose, s_xhi, s_xlo = sem("s_xpose"), sem("s_xhi"), sem("s_xlo")
        s_rt = sem("s_rt")
        s_logit, s_lcopy, s_lmax, s_lexp = sem("s_logit"), sem("s_lcopy"), sem("s_lmax"), sem("s_lexp")
        s_dense, s_dT, s_dTcopy, s_dram = sem("s_dense"), sem("s_dT"), sem("s_dTcopy"), sem("s_dram")
        s_gate, s_up, s_down = sem("s_gate"), sem("s_up"), sem("s_down")
        s_silu, s_weighted, s_h, s_hhi, s_hlo = (sem("s_silu"), sem("s_weighted"), sem("s_h"), sem("s_hhi"),
                                                 sem("s_hlo"))
        s_nb, s_bias, s_attw = sem("s_nb"), sem("s_bias"), sem("s_attw")
        s_z, s_G, s_Gc, s_X, s_Xc, s_S = sem("s_z"), sem("s_G"), sem("s_Gc"), sem("s_X"), sem("s_Xc"), sem("s_S")
        s_smax, s_exp, s_w, s_M, s_Mc, s_P, s_Pc = (sem("s_smax"), sem("s_exp"), sem("s_w"), sem("s_M"),
                                                    sem("s_Mc"), sem("s_P"), sem("s_Pc"))
        s_xcur, s_base, s_U, s_attn = sem("s_xcur"), sem("s_base"), sem("s_U"), sem("s_attn")
        s_y, s_yT, s_comb, s_res = sem("s_y"), sem("s_yT"), sem("s_comb"), sem("s_res")
        N_CONST = 11

        x_v = x.rearrange("b (p j) d -> b p j d", j=CH)
        out_v = out.rearrange("b (p j) d -> b p j d", j=CH)
        w_v = w_all.rearrange("p n k m -> p (n k m)")
        w_hi_v = w_hi[:, :, :, :].rearrange("p n k m -> p (n k m)")
        w_lo_v = w_lo[:, :, :, :].rearrange("p n k m -> p (n k m)")
        CW = CHUNK * 3 * P

        def tile_cols(buf, t):
            return buf[:, bass.ds(t * L, L)]

        block = ctx.enter_context(nc.Block())

        @block.sync
        def _(sp):
            def load_weights(c):
                if c >= STAGES:
                    sp.wait_ge(s_wlo, c - STAGES + 1)
                sp.dma_start(stage[:, c % STAGES, :], w_v[:, c * CW:(c + 1) * CW]).then_inc(s_wload[c % STAGES], 16)

            def load_pattern(t, q, first):
                slot = q % SLOTS
                if q == 0:
                    sp.wait_ge(s_dram, 16 if first else 32)
                if q >= SLOTS:
                    sp.wait_ge(s_weighted, t * NB + last_block[q - SLOTS] + 1)
                elif not first:
                    sp.wait_ge(s_weighted, t * NB + (last_block[q - SLOTS + len(patterns)] + 1 - NB))
                for e, a, b in patterns[q]:
                    src = dense_dram[bass.ds(t * E + e, 1), :].broadcast_to([b - a, L])
                    sp.dma_start(route[a:b, slot, :], src).then_inc(s_route[slot], 16)

            sp.dma_start(xn[:, 0:CH, :], x_v[0]).then_inc(s_x[0], 16)
            load_weights(0)
            load_weights(1)
            for b in range(1, B):
                sp.dma_start(xn[:, b * CH:(b + 1) * CH, :], x_v[b]).then_inc(s_x[b], 16)
            for c in range(STAGES, AHEAD + 1):
                load_weights(c)
            for q in range(SLOTS):
                load_pattern(0, q, True)
            for n in range(NB):
                if n % CHUNK == 0 and n // CHUNK + AHEAD + 1 < NCHUNK:
                    load_weights(n // CHUNK + AHEAD + 1)
                for q in range(SLOTS, len(patterns)):
                    if last_block[q - SLOTS] == n:
                        load_pattern(0, q, True)
            with sp.Fori(1, B) as t:
                for q in range(len(patterns)):
                    load_pattern(t, q, False)

        @block.tensor
        def _(pe):
            def product(dst, lhi, llo, rhi, rlo, start, stop):
                nc.tensor.matmul(dst, lhi, rhi, start=start, stop=False)
                nc.tensor.matmul(dst, lhi, rlo, start=False, stop=False)
                return nc.tensor.matmul(dst, llo, rhi, start=False, stop=stop)

            def gate_up(t, n, first):
                if first and n % CHUNK == 0:
                    pe.wait_ge(s_wlo, n // CHUNK + 1)
                xh, xl = tile_cols(xT_hi, t), tile_cols(xT_lo, t)
                dt, m = prev(n, RING)
                if not (first and dt < 0):
                    pe.wait_ge(s_silu, t * NB + (dt * NB + m + 1))
                product(gate_ps[n % RING], w_hi[:, n, 0, :], w_lo[:, n, 0, :], xh, xl, True, True).then_inc(s_gate, 1)
                if not (first and dt < 0):
                    pe.wait_ge(s_hlo, t * NB + (dt * NB + m + 1))
                product(up_ps[n % RING], w_hi[:, n, 1, :], w_lo[:, n, 1, :], xh, xl, True, True).then_inc(s_up, 1)

            def down(t, m, first):
                if m == 0 and not first:
                    pe.wait_ge(s_y, t)
                pe.wait_ge(s_hlo, t * NB + m + 1)
                product(ffn_ps, w_hi[:, m, 2, :], w_lo[:, m, 2, :], h_hi[:, m % RING, :], h_lo[:, m % RING, :],
                        m == 0, m == NB - 1).then_inc(s_down, 1)

            def transpose_x(b):
                pe.wait_ge(s_ln, b + 1)
                if b == 0:
                    pe.wait_ge(s_ident, 1)
                for j in range(CH):
                    last = nc.tensor.transpose(misc[:, j * P:(j + 1) * P], xn[:, b * CH + j, :], ident[:, :])
                last.then_inc(s_xpose, 1)

            def router(b):
                pe.wait_ge(s_xlo, b + 1)
                if b == 0:
                    pe.wait_ge(s_rt, 2)
                for j in range(CH):
                    c = slice((b * CH + j) * P, (b * CH + j + 1) * P)
                    last = product(misc[:, j * E:(j + 1) * E], xT_hi[:, c], xT_lo[:, c], rt_hi[:, :], rt_lo[:, :],
                                   True, True)
                last.then_inc(s_logit, 1)

            def dense_transpose(first):
                pe.wait_ge(s_dense, 1 if first else 2)
                for k in range(1 if first else B - 1):
                    last = nc.tensor.transpose(misc[0:E * CH, k * P:(k + 1) * P],
                                               dense[:, k, :, :].rearrange("p e j -> p (e j)"), ident[:, :])
                last.then_inc(s_dT, 1)

            def bias_products():
                pe.wait_ge(s_const, 16 * N_CONST)
                pe.wait_ge(s_nb, 1)
                nc.tensor.matmul(misc[0:1, 0:2 * D], cols[:, 1:2], wqkv_raw[:, 0:2 * D], start=True, stop=True)
                nc.tensor.matmul(misc[:, 2 * D:3 * D], nb_bc[:, :], wqkv_raw[:, D:2 * D], start=True, stop=True)
                nc.tensor.matmul(misc[:, 3 * D:4 * D], wqkv_raw[:, 2 * D:3 * D], nb_bc[:, :], start=True,
                                 stop=True).then_inc(s_bias, 1)

            def att_gram(t):
                pe.wait_ge(s_z, 2 * t + 2)
                for j in range(CH):
                    last = nc.tensor.matmul(misc[:, 0:D + 1], z[:, j, 0:D], z[:, j, 0:D + 1], start=(j == 0),
                                            stop=(j == CH - 1))
                last.then_inc(s_G, 1)

            def att_keys(t):
                pe.wait_ge(s_Gc, t + 1)
                nc.tensor.matmul(misc[:, 0:D], mat_a[:, 0:D], wqkT[:, D:2 * D], start=True, stop=True)
                nc.tensor.matmul(misc[0:1, D:2 * D], mat_a[:, D:D + 1], wqkT[:, D:2 * D], start=True,
                                 stop=True).then_inc(s_X, 1)

            def att_scores(t):
                pe.wait_ge(s_Xc, 2 * t + 2)
                nc.tensor.matmul(misc[:, 0:D], wqkT[:, 0:D], mat_b, start=True, stop=False)
                nc.tensor.matmul(misc[:, 0:D], bqk_row[0:1, 0:D], r_row[0:1, :], start=False,
                                 stop=True).then_inc(s_S, 1)

            def att_mix(t):
                pe.wait_ge(s_w, t + 1)
                nc.tensor.matmul(misc[:, 0:D], mat_a[:, 0:D], proj_sb[:, :], start=True, stop=True).then_inc(s_M, 1)

            def att_fold(t):
                pe.wait_ge(s_Mc, t + 1)
                nc.tensor.matmul(misc[:, 0:D], wv_n[:, :], mat_b, start=True, stop=True)
                nc.tensor.matmul(misc[:, D:2 * D], bv_bc[:, :], mat_b, start=True, stop=True).then_inc(s_P, 1)

            def att_out(t):
                pe.wait_ge(s_Pc, 2 * t + 2)
                pe.wait_ge(s_xcur, t + 1)
                for j in range(CH):
                    last = nc.tensor.matmul(misc[:, j * D:(j + 1) * D], x_cur[:, j * P:(j + 1) * P], mat_a[:, 0:D],
                                            start=True, stop=True)
                last.then_inc(s_U, 1)

            def attention(t, n, n0):
                if n == n0:
                    att_gram(t)
                if n == n0 + 2:
                    att_keys(t)
                if n == n0 + 4:
                    att_scores(t)
                if n == n0 + 8:
                    att_mix(t)
                if n == n0 + 10:
                    att_fold(t)
                if n == n0 + 12:
                    att_out(t)

            def final_transpose(t1):
                pe.wait_ge(s_y, t1)
                pe.wait_ge(s_attn, t1)
                for j in range(CH):
                    last = nc.tensor.transpose(misc[:, j * P:(j + 1) * P], yT[:, j * P:(j + 1) * P], ident[:, :])
                last.then_inc(s_yT, 1)

            transpose_x(0)
            router(0)
            for n in range(NB):
                gate_up(0, n, True)
                if n >= LAG:
                    down(0, n - LAG, True)
                if n == 0:
                    pe.wait_ge(s_lcopy, 1)
                    dense_transpose(True)
                if n == 2:
                    pe.wait_ge(s_dTcopy, 1)
                    bias_products()
                if n == 4:
                    pe.wait_ge(s_attw, 5)
                if n in (4, 7, 10):
                    if n > 4:
                        pe.wait_ge(s_lcopy, n // 3)
                    transpose_x(n // 3)
                if n in (5, 8, 11):
                    router(n // 3)
                if n == 17:
                    pe.wait_ge(s_lcopy, B)
                    dense_transpose(False)
                if n == 20:
                    pe.wait_ge(s_dTcopy, 2)
                attention(0, n, 20)
            with pe.Fori(1, B) as t:
                for n in range(NB):
                    gate_up(t, n, False)
                    if n < LAG:
                        down(t - 1, NB + n - LAG, False)
                    else:
                        down(t, n - LAG, False)
                    if n == 4:
                        final_transpose(t)
                    if n == 8:
                        pe.wait_ge(s_comb, t)
                    attention(t, n, 8)
            for m in range(NB - LAG, NB):
                down(B - 1, m, False)
            final_transpose(B)

        @block.scalar
        def _(act):
            def split_hi(c):
                act.wait_ge(s_wload[c % STAGES], 16 * (c // STAGES + 1))
                nc.scalar.copy(w_hi_v[:, c * CW:(c + 1) * CW], stage[:, c % STAGES, :]).then_inc(s_whi, 1)

            def silu(t, n, first):
                dt, m = prev(n, RING)
                if not (first and dt < 0):
                    act.wait_ge(s_h, t * NB + (dt * NB + m + 1))
                act.wait_ge(s_gate, t * NB + n + 1)
                nc.scalar.activation(s_buf[:, n % RING, :], gate_ps[n % RING], ACT.Silu).then_inc(s_silu, 1)

            def round_h(t, m, first):
                dt, k = prev(m, RING)
                if not (first and dt < 0):
                    act.wait_ge(s_down, t * NB + (dt * NB + k + 1))
                act.wait_ge(s_h, t * NB + m + 1)
                nc.scalar.copy(h_hi[:, m % RING, :], up_ps[m % RING]).then_inc(s_hhi, 1)

            def round_x(b):
                act.wait_ge(s_xpose, b + 1)
                nc.scalar.copy(xT_hi[:, b * L:(b + 1) * L], misc).then_inc(s_xhi, 1)

            def router_exp(first):
                act.wait_ge(s_lmax, 1 if first else 2)
                k = CH if first else NR
                nc.scalar.activation(ex[:, 0:k, :], ex[:, 0:k, :], ACT.Exp).then_inc(s_lexp, 1)

            def store_dense(first):
                act.wait_ge(s_dTcopy, 1 if first else 2)
                lo, hi = (0, 1) if first else (1, B)
                dst = dense_dram.rearrange("(b e) (j p) -> (e j) b p", b=B, j=CH)[:, lo:hi, :]
                act.dma_start(dst, denseT[:, 0:(hi - lo) * P].rearrange("q (b p) -> q b p", p=P)).then_inc(s_dram, 16)

            def att_exp(t):
                act.wait_ge(s_smax, t + 1)
                nc.scalar.activation(mat_a[:, 0:D], misc[:, 0:D], ACT.Exp, bias=sm[:, 1:2], scale=SCALE,
                                     accum_out=sm[:, 2:3]).then_inc(s_exp, 1)

            def ffn_silu(t1):
                act.wait_ge(s_down, t1 * NB)
                nc.scalar.activation(yT, ffn_ps, ACT.Silu).then_inc(s_y, 1)

            def load_again(t):
                act.dma_start(x_again, x_v[bass.ds(t, 1)].rearrange("b p j d -> (b p) j d")).then_inc(s_xagain, 16)

            def store(t):
                act.wait_ge(s_res, t + 1)
                act.dma_start(out_v[bass.ds(t, 1)].rearrange("b p j d -> (b p) j d"), o_sb).then_inc(s_out, 16)

            act.dma_start(rt_raw[:, :], routerT).then_inc(s_rtc, 16)
            act.dma_start(cols[:, 0:1], norm_w.rearrange("(p o) -> p o", o=1)).then_inc(s_const, 16)
            act.dma_start(cols[:, 1:2], norm_b.rearrange("(p o) -> p o", o=1)).then_inc(s_const, 16)
            act.dma_start(cols[:, 2:3], qkv_b[2 * D:3 * D].rearrange("(p o) -> p o", o=1)).then_inc(s_const, 16)
            act.dma_start(wqkv_raw[:, :], wqkvT).then_inc(s_const, 16)
            act.dma_start(wv_n[:, :], wv).then_inc(s_const, 16)
            act.dma_start(proj_sb[:, :], projT).then_inc(s_const, 16)
            row = lambda v: v.rearrange("(o d) -> o d", o=1)
            act.dma_start(nw_bc[:, :], row(norm_w).broadcast_to([P, D])).then_inc(s_const, 16)
            act.dma_start(bk_bc[:, :], row(qkv_b[D:2 * D]).broadcast_to([P, D])).then_inc(s_const, 16)
            act.dma_start(pb_bc[:, :], row(proj_b).broadcast_to([P, D])).then_inc(s_const, 16)
            act.dma_start(bqk_row[:, :], row(qkv_b[0:2 * D])).then_inc(s_const, 16)
            act.dma_start(bkL_row[:, :], row(qkv_b[D:2 * D])).then_inc(s_const, 16)
            split_hi(0)
            split_hi(1)
            round_x(0)
            router_exp(True)
            for c in range(STAGES, AHEAD):
                split_hi(c)
            store_dense(True)
            for n in range(NB):
                if n % CHUNK == 0 and n // CHUNK + AHEAD < NCHUNK:
                    split_hi(n // CHUNK + AHEAD)
                silu(0, n, True)
                if n >= 1:
                    round_h(0, n - 1, True)
                if n in (5, 8, 11):
                    round_x(n // 3)
                if n == 15:
                    router_exp(False)
                if n == 18:
                    store_dense(False)
                if n == 20 + 6:
                    att_exp(0)
            act.wait_ge(s_wlo, NCHUNK)
            load_again(0)
            with act.Fori(1, B) as t:
                for n in range(NB):
                    silu(t, n, False)
                    if n == 0:
                        round_h(t - 1, NB - 1, False)
                    else:
                        round_h(t, n - 1, False)
                    if n == LAG:
                        ffn_silu(t)
                    if n == 8 + 6:
                        att_exp(t)
                    if n == 10:
                        store(t - 1)
                    if n == 11:
                        load_again(t)
            round_h(B - 1, NB - 1, False)
            ffn_silu(B)
            store(B - 1)
            act.wait_ge(s_out, 16 * B)

        @block.gpsimd
        def _(pool):
            count = [0]

            def step(ins):
                count[0] += 1
                ins.then_inc(s_pool, 1)
                pool.wait_ge(s_pool, count[0])

            def weigh(t, n, first):
                q = pattern_of[n]
                if n == 0 or pattern_of[n - 1] != q:
                    k = q // SLOTS + 1
                    step16 = slot_step[q % SLOTS]
                    pool.wait_ge(s_route[q % SLOTS], t * (ROUNDS * step16) + k * step16)
                pool.wait_ge(s_silu, t * NB + n + 1)
                s = s_buf[:, n % RING, :]
                nc.gpsimd.tensor_tensor(s, s, route[:, q % SLOTS, :], ALU.mult).then_inc(s_weighted, 1)

            def inverse_roots(b):
                pool.wait_ge(s_var, 2 * b + 1)
                nc.gpsimd.tensor_tensor(rstd[:, :], ve[:, 0:CH], mhalf[:, :], ALU.pow).then_inc(s_rstd, 1)
                pool.wait_ge(s_var, 2 * b + 2)
                nc.gpsimd.tensor_tensor(r2[:, b * CH:(b + 1) * CH], ve[:, CH:2 * CH], mhalf[:, :],
                                        ALU.pow).then_inc(s_r2, 1)

            step(nc.gpsimd.memset(ident[:, :], 0.0))
            nc.gpsimd.affine_select(out=ident[:, :], in_=ident[:, :], compare_op=ALU.not_equal, fill=1.0, base=0,
                                    pattern=[[-1, P]], channel_multiplier=1).then_inc(s_ident, 1)
            step(nc.gpsimd.memset(mhalf[:, :], -0.5))
            inverse_roots(0)
            pool.wait_ge(s_const, 16 * N_CONST)
            nc.gpsimd.tensor_tensor(wv_n[:, :], wv_n[:, :], nw_bc[:, :], ALU.mult).then_inc(s_attw, 1)
            for n in range(NB):
                weigh(0, n, True)
                if n in (2, 5, 8):
                    inverse_roots(n // 3 + 1)
            with pool.Fori(1, B) as t:
                for n in range(NB):
                    weigh(t, n, False)

        @block.vector
        def _(dve):
            count = [0]

            def step(ins):
                count[0] += 1
                ins.then_inc(s_dve, 1)
                dve.wait_ge(s_dve, count[0])

            def layer_norm(b):
                dve.wait_ge(s_x[b], 16)
                xb = xn[:, b * CH:(b + 1) * CH, :]
                for j in range(CH):
                    last = nc.vector.bn_stats(stats[:, j, :], xb[:, j, :])
                step(last)
                for j in range(CH):
                    last = nc.vector.bn_aggr(mv[:, j, :], stats[:, j, :])
                step(last)
                nc.vector.tensor_scalar(ve[:, 0:CH], mv[:, :, 1], LN_EPS, None, ALU.add).then_inc(s_var, 1)
                dve.wait_ge(s_rstd, b + 1)
                step(nc.vector.tensor_tensor(ve[:, CH:2 * CH], mv[:, :, 1], rstd[:, :], ALU.mult))
                step(nc.vector.tensor_tensor(ve[:, CH:2 * CH], ve[:, CH:2 * CH], rstd[:, :], ALU.mult))
                nc.vector.tensor_scalar(ve[:, CH:2 * CH], ve[:, CH:2 * CH], LN_EPS, None, ALU.add).then_inc(s_var, 1)
                for j in range(CH):
                    last = nc.vector.tensor_scalar(xb[:, j, :], xb[:, j, :], mv[:, j, 0:1], rstd[:, j:j + 1],
                                                   ALU.subtract, ALU.mult)
                last.then_inc(s_ln, 1)
                dve.wait_ge(s_ln, b + 1)

            def split_x(b):
                dve.wait_ge(s_xhi, b + 1)
                c = slice(b * L, (b + 1) * L)
                nc.vector.tensor_tensor(xT_lo[:, c], misc, xT_hi[:, c].bitcast(F32), ALU.subtract).then_inc(s_xlo, 1)

            def copy_logits(b):
                k = max(b - 1, 0) * CH
                dve.wait_ge(s_logit, b + 1)
                nc.vector.tensor_copy(lg[:, k:k + CH, :], misc[:, 0:CH * E].rearrange("p (j e) -> p j e", e=E)
                                      ).then_inc(s_lcopy, 1)

            def pick_top(k0, k):
                for j in range(k0, k0 + k):
                    last = nc.vector.max(top8[:, j, :], lg[:, j, :])
                step(last)
                for j in range(k0, k0 + k):
                    last = nc.vector.match_replace(lr[:, j, :], top8[:, j, :], lg[:, j, :], NEG)
                step(last)

            def shift_logits(k):
                nc.vector.tensor_tensor(ex[:, 0:k, :], lg[:, 0:k, :], top8[:, 0:k, 0:1].broadcast_to([P, k, E]),
                                        ALU.subtract).then_inc(s_lmax, 1)

            def dense_weights(first):
                k = CH if first else NR
                step(nc.vector.tensor_tensor(lr[:, 0:k, :], lr[:, 0:k, :], lg[:, 0:k, :], ALU.not_equal))
                dve.wait_ge(s_lexp, 1 if first else 2)
                step(nc.vector.tensor_tensor(ex[:, 0:k, :], ex[:, 0:k, :], lr[:, 0:k, :], ALU.mult))
                step(nc.vector.tensor_reduce(rsum[:, 0:k], ex[:, 0:k, :], AX_X, ALU.add))
                step(nc.vector.reciprocal(rsum[:, NR:NR + k], rsum[:, 0:k]))
                for b in range(k // CH):
                    j = slice(b * CH, (b + 1) * CH)
                    last = nc.vector.tensor_tensor(
                        dense[:, b, :, :].rearrange("p e j -> p j e"), ex[:, j, :],
                        rsum[:, NR + b * CH:NR + (b + 1) * CH].unsqueeze(2).broadcast_to([P, CH, E]), ALU.mult)
                last.then_inc(s_dense, 1)

            def copy_denseT(first):
                k = 1 if first else B - 1
                dve.wait_ge(s_dT, 1 if first else 2)
                nc.vector.tensor_copy(denseT[:, 0:k * P], misc[0:E * CH, 0:k * P]).then_inc(s_dTcopy, 1)

            def split_lo(c):
                dve.wait_ge(s_whi, c + 1)
                nc.vector.tensor_tensor(w_lo_v[:, c * CW:(c + 1) * CW], stage[:, c % STAGES, :],
                                        w_hi_v[:, c * CW:(c + 1) * CW].bitcast(F32), ALU.subtract).then_inc(s_wlo, 1)

            def hidden(t, n):
                dve.wait_ge(s_up, t * NB + n + 1)
                dve.wait_ge(s_weighted, t * NB + n + 1)
                nc.vector.tensor_tensor(up_ps[n % RING], s_buf[:, n % RING, :], up_ps[n % RING],
                                        ALU.mult).then_inc(s_h, 1)

            def split_h(t, m, first):
                dve.wait_ge(s_hhi, t * NB + m + 1)
                nc.vector.tensor_tensor(h_lo[:, m % RING, :], up_ps[m % RING], h_hi[:, m % RING, :].bitcast(F32),
                                        ALU.subtract).then_inc(s_hlo, 1)

            def attention_weights():
                dve.wait_ge(s_bias, 1)
                nc.vector.tensor_tensor(bqk_row[:, :], misc[0:1, 0:2 * D], bqk_row[:, :], ALU.add).then_inc(s_attw, 1)
                step(nc.vector.tensor_tensor(bkL_row[:, :], misc[0:1, D:2 * D], bkL_row[:, :], ALU.add))
                step(nc.vector.tensor_scalar(bkL_row[:, :], bkL_row[:, :], float(L), None, ALU.mult))
                nc.vector.tensor_tensor(bk_bc[:, :], misc[:, 2 * D:3 * D], bk_bc[:, :], ALU.add).then_inc(s_attw, 1)
                nc.vector.tensor_scalar(bv_bc[:, :], misc[:, 3 * D:4 * D], cols[:, 2:3], None,
                                        ALU.add).then_inc(s_attw, 1)

            def att_copy_gram(t):
                dve.wait_ge(s_G, t + 1)
                nc.vector.tensor_copy(mat_a, misc[:, 0:D + 1]).then_inc(s_Gc, 1)

            def att_copy_keys(t):
                dve.wait_ge(s_X, t + 1)
                nc.vector.scalar_tensor_tensor(out=mat_b, in0=bk_bc[:, :], scalar=mat_a[:, D:D + 1],
                                               in1=misc[:, 0:D], op0=ALU.mult, op1=ALU.add).then_inc(s_Xc, 1)
                nc.vector.tensor_tensor(r_row[:, :], misc[0:1, D:2 * D], bkL_row[:, :], ALU.add).then_inc(s_Xc, 1)

            def att_max(t, t2):
                dve.wait_ge(s_S, t + 1)
                nc.vector.tensor_reduce(sm[:, 0:1], misc[:, 0:D], AX_X, ALU.max).then_inc(s_dve, 1)
                dve.wait_ge(s_dve, t2 + 2)
                nc.vector.tensor_scalar(sm[:, 1:2], sm[:, 0:1], -SCALE, None, ALU.mult).then_inc(s_smax, 1)

            def att_normalise(t, t2):
                dve.wait_ge(s_exp, t + 1)
                nc.vector.reciprocal(sm[:, 3:4], sm[:, 2:3]).then_inc(s_dve, 1)
                dve.wait_ge(s_dve, t2 + 3)
                nc.vector.tensor_scalar(mat_a[:, 0:D], mat_a[:, 0:D], sm[:, 3:4], None, ALU.mult).then_inc(s_w, 1)

            def att_copy_mix(t):
                dve.wait_ge(s_M, t + 1)
                nc.vector.tensor_copy(mat_b, misc[:, 0:D]).then_inc(s_Mc, 1)

            def att_copy_fold(t):
                dve.wait_ge(s_P, t + 1)
                nc.vector.tensor_copy(mat_a[:, 0:D], misc[:, 0:D]).then_inc(s_Pc, 1)
                nc.vector.tensor_tensor(out_bias, misc[:, D:2 * D], pb_bc[:, :], ALU.add).then_inc(s_Pc, 1)

            def att_finish(t):
                dve.wait_ge(s_U, t + 1)
                dve.wait_ge(s_base, t + 1)
                for j in range(CH):
                    v = xn[:, bass.ds(t * CH + j, 1), :].rearrange("p o d -> p (o d)")
                    last = nc.vector.scalar_tensor_tensor(out=v, in0=misc[:, j * D:(j + 1) * D],
                                                          scalar=r2_cur[:, j:j + 1], in1=v, op0=ALU.mult, op1=ALU.add)
                last.then_inc(s_attn, 1)

            def make_z(t, t2):
                nc.vector.tensor_copy(r2_cur[:, :], r2[:, bass.ds(t * CH, CH)]).then_inc(s_dve, 1)
                nc.vector.memset(z[:, :, D:D + 1], 1.0).then_inc(s_z, 1)
                dve.wait_ge(s_dve, t2 + 1)
                nc.vector.tensor_tensor(z[:, :, 0:D], xn[:, bass.ds(t * CH, CH), :],
                                        r2_cur[:, :].unsqueeze(2).broadcast_to([P, CH, D]), ALU.mult).then_inc(s_z, 1)

            def make_x_cur(t):
                nc.vector.tensor_tensor(x_cur, tile_cols(xT_hi, t).bitcast(F32), tile_cols(xT_lo, t).bitcast(F32),
                                        ALU.add).then_inc(s_xcur, 1)

            def add_bias(t):
                dve.wait_ge(s_Pc, 2 * t + 2)
                v = xn[:, bass.ds(t * CH, CH), :]
                nc.vector.tensor_tensor(v, v, out_bias.unsqueeze(1).broadcast_to([P, CH, D]), ALU.add).then_inc(s_base, 1)

            def attention(t, t2, n, n0):
                if n == n0 - 1:
                    make_z(t, t2)
                if n == n0 + 1:
                    att_copy_gram(t)
                    make_x_cur(t)
                if n == n0 + 12:
                    add_bias(t)
                if n == n0 + 3:
                    att_copy_keys(t)
                if n == n0 + 5:
                    att_max(t, t2)
                if n == n0 + 7:
                    att_normalise(t, t2)
                if n == n0 + 9:
                    att_copy_mix(t)
                if n == n0 + 11:
                    att_copy_fold(t)
                if n == n0 + 13:
                    att_finish(t)

            def combine(t):
                dve.wait_ge(s_yT, t + 1)
                dve.wait_ge(s_xagain, 16 * t + 16)
                if not isinstance(t, int) or t > 0:
                    dve.wait_ge(s_out, 16 * t)
                nc.vector.tensor_tensor(o_sb, misc.rearrange("p (j d) -> p j d", j=CH),
                                        xn[:, bass.ds(t * CH, CH), :], ALU.mult).then_inc(s_comb, 1)
                dve.wait_ge(s_comb, t + 1)
                nc.vector.tensor_tensor(o_sb, o_sb, x_again, ALU.add).then_inc(s_res, 1)

            dve.wait_ge(s_rtc, 16)
            nc.vector.tensor_copy(rt_hi[:, :], rt_raw[:, :]).then_inc(s_rt, 1)
            dve.wait_ge(s_rt, 1)
            nc.vector.tensor_tensor(rt_lo[:, :], rt_raw[:, :], rt_hi[:, :].bitcast(F32),
                                    ALU.subtract).then_inc(s_rt, 1)
            layer_norm(0)
            split_x(0)
            copy_logits(0)
            dve.wait_ge(s_lcopy, 1)
            pick_top(0, CH)
            shift_logits(CH)
            dense_weights(True)
            for c in range(2):
                split_lo(c)
            copy_denseT(True)
            for c in range(2, AHEAD):
                split_lo(c)
            dve.wait_ge(s_const, 16 * N_CONST)
            step(nc.vector.memset(nb_bc[:, :], 1.0))
            nc.vector.tensor_scalar(nb_bc[:, :], nb_bc[:, :], cols[:, 1:2], None, ALU.mult).then_inc(s_nb, 1)
            nc.vector.tensor_scalar(wqkT[:, :], wqkv_raw[:, 0:2 * D], cols[:, 0:1], None, ALU.mult).then_inc(s_attw, 1)
            for n in range(NB):
                if n % CHUNK == 0 and n // CHUNK + AHEAD < NCHUNK:
                    split_lo(n // CHUNK + AHEAD)
                hidden(0, n)
                if n >= 1:
                    split_h(0, n - 1, True)
                if n == 3:
                    attention_weights()
                if n in (2, 5, 8):
                    layer_norm(n // 3 + 1)
                if n in (5, 8, 11):
                    split_x(n // 3)
                if n == 6:
                    dve.wait_ge(s_dram, 16)
                if n in (6, 9, 12):
                    copy_logits(n // 3 - 1)
                if n == 12:
                    dve.wait_ge(s_lcopy, B)
                if n in (12, 13, 14):
                    pick_top((n - 12) * CH, CH)
                if n == 14:
                    shift_logits(NR)
                if n == 16:
                    dense_weights(False)
                if n == 18:
                    copy_denseT(False)
                if n == 19:
                    dve.wait_ge(s_r2, B)
                    dve.wait_ge(s_dram, 32)
                attention(0, count[0], n, 20)
            base = count[0]
            with dve.Fori(1, B) as t:
                for n in range(NB):
                    hidden(t, n)
                    if n == 0:
                        split_h(t - 1, NB - 1, False)
                    else:
                        split_h(t, n - 1, False)
                    if n == 5:
                        combine(t - 1)
                    attention(t, t * 3 + base, n, 8)
            split_h(B - 1, NB - 1, False)
            combine(B - 1)


def kernel(L0_attn_x, L0_attn_norm_w, L0_attn_norm_b, L0_attn_qkv_w, L0_attn_qkv_b, L0_attn_proj_w, L0_attn_proj_b,
           L0_ffn_router_w, L0_ffn_gate_w, L0_ffn_up_w, L0_ffn_down_w):
    import numpy as np
    import concourse.bacc as bacc
    from concourse.bass_utils import run_bass_kernel_spmd

    x = np.asarray(L0_attn_x)
    B, L, D = x.shape
    qkv_w = np.asarray(L0_attn_qkv_w)
    E, F, H = L0_ffn_gate_w.shape
    NB = E * F // P
    gate = np.asarray(L0_ffn_gate_w).reshape(NB, P, H).transpose(2, 0, 1)
    up = np.asarray(L0_ffn_up_w).reshape(NB, P, H).transpose(2, 0, 1)
    down = np.asarray(L0_ffn_down_w).transpose(0, 2, 1).reshape(NB, P, H).transpose(1, 0, 2)
    arrays = {
        "x": x, "norm_w": np.asarray(L0_attn_norm_w), "norm_b": np.asarray(L0_attn_norm_b),
        "wqkvT": qkv_w.T, "wv": qkv_w[2 * D:], "qkv_b": np.asarray(L0_attn_qkv_b),
        "projT": np.asarray(L0_attn_proj_w).T, "proj_b": np.asarray(L0_attn_proj_b),
        "routerT": np.asarray(L0_ffn_router_w).T, "w_all": np.stack([gate, up, down], axis=2),
    }
    arrays = {k: np.ascontiguousarray(v) for k, v in arrays.items()}
    nc = bacc.Bacc("TRN2", target_bir_lowering=False, num_devices=1)
    args = [nc.dram_tensor(k, v.shape, F32, kind="ExternalInput").ap() for k, v in arrays.items()]
    dense = nc.dram_tensor("dense_w", (B * E, L), F32, kind="Internal").ap()
    out = nc.dram_tensor("out", (B, L, D), F32, kind="ExternalOutput").ap()
    gated_block(nc, *args, dense, out)
    r = run_bass_kernel_spmd(nc, [arrays], core_ids=[0])
    return r.results[0]["out"]
```

```python
from contextlib import ExitStack

import concourse.bass as bass
from concourse import mybir

F32 = mybir.dt.float32
F32R = mybir.dt.float32r
ALU = mybir.AluOpType
ACT = mybir.ActivationFunctionType
AX_X = mybir.AxisListType.X

P = 128
LN_EPS = 1e-5
TOP_K = 8
LAG = 4
G_RING = 2
U_RING = 4
S_RING = 3
H_RING = 4
ROUND_LAG = 2
CHUNK = 2
STAGES = 3
AHEAD = 5
NEG = -3.4028235e38


def block_pattern(n, per_expert):
    out, f = [], n * P
    while f < (n + 1) * P:
        e = f // per_expert
        end = min((e + 1) * per_expert, (n + 1) * P)
        out.append((e, f - n * P, end - n * P))
        f = end
    return out


def gated_block(nc, x, columns, rows, routerT, w_all, dense_dram, out):
    B, L, D = x.shape
    E = routerT.shape[1]
    NB = w_all.shape[1]
    FE = NB * P // E
    CH = L // P
    NCHUNK = NB // CHUNK
    SCALE = float(L) ** -0.5
    assert D == P and L == 512 and NB % CHUNK == 0 and E * CH <= P

    patterns, pattern_of = [], []
    for n in range(NB):
        cut = block_pattern(n, FE)
        if not patterns or patterns[-1] != cut:
            patterns.append(cut)
        pattern_of.append(len(patterns) - 1)
    last_block = [max(n for n in range(NB) if pattern_of[n] == q) for q in range(len(patterns))]
    SLOTS = 4
    assert len(patterns) % SLOTS == 0

    def loads(q):
        return 16 * sum(len(patterns[k]) for k in range(q % SLOTS, q + 1, SLOTS))

    def prev(n, depth):
        if n >= depth:
            return 0, n - depth
        return -1, max(m for m in range(NB) if m % depth == n % depth)

    with ExitStack() as ctx:
        def sb(name, shape, dt=F32):
            return ctx.enter_context(nc.sbuf_tensor(name, shape, dt))

        def sem(name):
            return ctx.enter_context(nc.semaphore(name))

        psum = ctx.enter_context(nc.psum_tensor("psum", [P, 8, 512], F32))
        gate_ps = [psum[:, r, :] for r in range(G_RING)]
        up_ps = [psum[:, G_RING + r, :] for r in range(U_RING)]
        ffn_ps = psum[:, 6, :]
        misc = psum[:, 7, :]
        bias_ps = up_ps[U_RING - 1]

        w_hi = sb("w_hi", [P, NB, 3, P], F32R)
        w_lo = sb("w_lo", [P, NB, 3, P], F32R)
        xT_hi = sb("xT_hi", [P, B * L], F32R)
        xT_lo = sb("xT_lo", [P, B * L], F32R)
        xn = sb("xn", [P, B * CH, D])
        route = sb("route", [P, SLOTS, L])
        s_buf = sb("s_buf", [P, S_RING, L])
        h_hi = sb("h_hi", [P, H_RING, L], F32R)
        h_lo = sb("h_lo", [P, H_RING, L], F32R)
        stage = sb("stage", [P, STAGES, CHUNK * 3 * P])
        tail = stage[:, :, :].rearrange("p s n -> p (s n)")
        assert STAGES * CHUNK * 3 * P >= 3 * L
        yT = tail[:, 0:L]
        o_sb = tail[:, L:2 * L].rearrange("p (j d) -> p j d", j=CH)
        x_again = tail[:, 2 * L:3 * L].rearrange("p (j d) -> p j d", j=CH)

        col_sb = sb("col_sb", [P, columns.shape[1]])
        wqkv_raw = col_sb[:, 0:3 * D]
        wqkT = col_sb[:, 0:2 * D]
        wv_n = col_sb[:, 3 * D:4 * D]
        proj_sb = col_sb[:, 4 * D:5 * D]
        nw_col, nb_col, bv_col = (col_sb[:, 5 * D + i:5 * D + i + 1] for i in range(3))
        row_sb = sb("row_sb", [P, rows.shape[1]])
        nw_bc, bk_bc, pb_bc = row_sb[:, 0:D], row_sb[:, 2 * D:3 * D], row_sb[:, 4 * D:5 * D]
        bq_row = row_sb[0:1, D:2 * D]
        nb_bc = sb("nb_bc", [P, P])
        bv_bc = sb("bv_bc", [P, P])
        ident = sb("ident", [P, P])
        bkL_row = sb("bkL_row", [1, D])
        r_row = sb("r_row", [1, D])
        rt_raw = sb("rt_raw", [P, E])
        rt_hi = sb("rt_hi", [P, E], F32R)
        rt_lo = sb("rt_lo", [P, E], F32R)
        stats = sb("stats", [P, CH, 6])
        mv = sb("mv", [P, B * CH, 2])
        ve = sb("ve", [P, B * CH])
        mhalf = sb("mhalf", [P, B * CH])
        rstd = sb("rstd", [P, B * CH])
        r2 = sb("r2", [P, B * CH])
        r2_cur = sb("r2_cur", [P, CH])
        sm = sb("sm", [P, 4])
        rsum = sb("rsum", [P, 2 * 3 * CH])

        scratch = sb("scratch", [P, 4 * 129 + 2 * 130 + P])
        z = scratch[:, 0:CH * 129].rearrange("p (j d) -> p j d", j=CH)
        x_cur = scratch[:, 0:L]
        mat_a = scratch[:, 516:516 + 129]
        mat_b = scratch[:, 646:646 + D]
        out_bias = scratch[:, 776:776 + D]
        NR = 3 * CH
        lg = scratch[:, 0:NR * E].rearrange("p (j e) -> p j e", e=E)
        lr = scratch[:, NR * E:2 * NR * E].rearrange("p (j e) -> p j e", e=E)
        ex = scratch[:, 2 * NR * E:3 * NR * E].rearrange("p (j e) -> p j e", e=E)
        dense = scratch[:, 3 * NR * E:4 * NR * E].rearrange("p (b e j) -> p b e j", e=E, j=CH)
        top8 = scratch[:, 4 * NR * E:4 * NR * E + NR * 8].rearrange("p (j k) -> p j k", k=8)
        denseT = scratch[0:E * CH, 0:3 * P]

        s_x = [sem(f"s_x{b}") for b in range(B)]
        s_const = sem("s_const")
        s_rtc = sem("s_rtc")
        s_wload = [sem(f"s_wload{i}") for i in range(STAGES)]
        s_whi, s_wlo_dve, s_wlo_pool = sem("s_whi"), sem("s_wlo_dve"), sem("s_wlo_pool")
        s_route = [sem(f"s_route{i}") for i in range(SLOTS)]
        s_xagain, s_out = sem("s_xagain"), sem("s_out")
        s_ident = sem("s_ident")
        s_dve = sem("s_dve")
        s_pool = sem("s_pool")
        s_var, s_rstd, s_ln, s_r2 = sem("s_var"), sem("s_rstd"), sem("s_ln"), sem("s_r2")
        s_xpose, s_xhi, s_xlo = sem("s_xpose"), sem("s_xhi"), sem("s_xlo")
        s_rt = sem("s_rt")
        s_logit, s_lcopy, s_lmax, s_lexp = sem("s_logit"), sem("s_lcopy"), sem("s_lmax"), sem("s_lexp")
        s_dense, s_dT, s_dTcopy, s_dram = sem("s_dense"), sem("s_dT"), sem("s_dTcopy"), sem("s_dram")
        s_gate, s_up, s_down = sem("s_gate"), sem("s_up"), sem("s_down")
        s_silu, s_weighted, s_h, s_hhi, s_hlo = (sem("s_silu"), sem("s_weighted"), sem("s_h"), sem("s_hhi"),
                                                 sem("s_hlo"))
        s_nb, s_bias, s_attw = sem("s_nb"), sem("s_bias"), sem("s_attw")
        s_z, s_G, s_Gc, s_X, s_Xc, s_S = sem("s_z"), sem("s_G"), sem("s_Gc"), sem("s_X"), sem("s_Xc"), sem("s_S")
        s_smax, s_exp, s_w, s_M, s_Mc, s_P, s_Pc = (sem("s_smax"), sem("s_exp"), sem("s_w"), sem("s_M"),
                                                    sem("s_Mc"), sem("s_P"), sem("s_Pc"))
        s_obias = sem("s_obias")
        s_xcur, s_base, s_U, s_attn = sem("s_xcur"), sem("s_base"), sem("s_U"), sem("s_attn")
        s_y, s_yT, s_comb, s_res = sem("s_y"), sem("s_yT"), sem("s_comb"), sem("s_res")
        N_CONST = 2
        ATT0, ATT = 30, 10

        x_v = x.rearrange("b (p j) d -> b p j d", j=CH)
        out_v = out.rearrange("b (p j) d -> b p j d", j=CH)
        w_v = w_all.rearrange("p n k m -> p (n k m)")
        w_hi_v = w_hi[:, :, :, :].rearrange("p n k m -> p (n k m)")
        w_lo_v = w_lo[:, :, :, :].rearrange("p n k m -> p (n k m)")
        CW = CHUNK * 3 * P

        def by_pool(c):
            return c % 3 == 1

        def wait_split(eng, c):
            own = by_pool(c)
            eng.wait_ge(s_wlo_pool if own else s_wlo_dve, sum(by_pool(k) == own for k in range(c + 1)))

        def split_lo(eng, c):
            eng.wait_ge(s_whi, c + 1)
            eng.tensor_tensor(w_lo_v[:, c * CW:(c + 1) * CW], stage[:, c % STAGES, :],
                              w_hi_v[:, c * CW:(c + 1) * CW].bitcast(F32), ALU.subtract
                              ).then_inc(s_wlo_pool if by_pool(c) else s_wlo_dve, 1)

        def tile_cols(buf, t):
            return buf[:, bass.ds(t * L, L)]

        block = ctx.enter_context(nc.Block())

        @block.sync
        def _(sp):
            def load_weights(c):
                if c >= STAGES:
                    wait_split(sp, c - STAGES)
                sp.dma_start(stage[:, c % STAGES, :], w_v[:, c * CW:(c + 1) * CW]).then_inc(s_wload[c % STAGES], 16)

            def load_pattern(t, q, first):
                slot = q % SLOTS
                if q == 0:
                    sp.wait_ge(s_dram, 16 if first else 32)
                if q >= SLOTS:
                    sp.wait_ge(s_weighted, t * NB + last_block[q - SLOTS] + 1)
                elif not first:
                    sp.wait_ge(s_weighted, t * NB + (last_block[q - SLOTS + len(patterns)] + 1 - NB))
                for e, a, b in patterns[q]:
                    src = dense_dram[bass.ds(t * E + e, 1), :].broadcast_to([b - a, L])
                    sp.dma_start(route[a:b, slot, :], src).then_inc(s_route[slot], 16)

            sp.dma_start(xn[:, 0:CH, :], x_v[0]).then_inc(s_x[0], 16)
            load_weights(0)
            for b in range(1, B):
                if b < STAGES:
                    load_weights(b)
                sp.dma_start(xn[:, b * CH:(b + 1) * CH, :], x_v[b]).then_inc(s_x[b], 16)
            assert B >= STAGES
            for c in range(STAGES, AHEAD):
                load_weights(c)
            for q in range(SLOTS):
                load_pattern(0, q, True)
            load_weights(AHEAD)
            for n in range(NB):
                if n % CHUNK == 0 and n // CHUNK + AHEAD + 1 < NCHUNK:
                    load_weights(n // CHUNK + AHEAD + 1)
                for q in range(SLOTS, len(patterns)):
                    if last_block[q - SLOTS] == n:
                        load_pattern(0, q, True)
            with sp.Fori(1, B) as t:
                for q in range(len(patterns)):
                    load_pattern(t, q, False)

        @block.tensor
        def _(pe):
            def product(dst, lhi, llo, rhi, rlo, start, stop):
                nc.tensor.matmul(dst, lhi, rhi, start=start, stop=False)
                nc.tensor.matmul(dst, lhi, rlo, start=False, stop=False)
                return nc.tensor.matmul(dst, llo, rhi, start=False, stop=stop)

            def gate_up(t, n, first):
                if first and n % CHUNK == 0:
                    wait_split(pe, n // CHUNK)
                xh, xl = tile_cols(xT_hi, t), tile_cols(xT_lo, t)
                dt, m = prev(n, G_RING)
                if not (first and dt < 0):
                    pe.wait_ge(s_silu, t * NB + (dt * NB + m + 1))
                product(gate_ps[n % G_RING], w_hi[:, n, 0, :], w_lo[:, n, 0, :], xh, xl, True, True).then_inc(s_gate, 1)
                dt, m = prev(n, U_RING)
                if not (first and dt < 0):
                    pe.wait_ge(s_hlo, t * NB + (dt * NB + m + 1))
                product(up_ps[n % U_RING], w_hi[:, n, 1, :], w_lo[:, n, 1, :], xh, xl, True, True).then_inc(s_up, 1)

            def down(t, m, first):
                if m == 0 and not first:
                    pe.wait_ge(s_y, t)
                pe.wait_ge(s_hlo, t * NB + m + 1)
                product(ffn_ps, w_hi[:, m, 2, :], w_lo[:, m, 2, :], h_hi[:, m % H_RING, :], h_lo[:, m % H_RING, :],
                        m == 0, m == NB - 1).then_inc(s_down, 1)

            def transpose_x(b):
                pe.wait_ge(s_ln, b + 1)
                if b == 0:
                    pe.wait_ge(s_ident, 1)
                for j in range(CH):
                    last = nc.tensor.transpose(misc[:, j * P:(j + 1) * P], xn[:, b * CH + j, :], ident[:, :])
                last.then_inc(s_xpose, 1)

            def router(b):
                pe.wait_ge(s_xlo, b + 1)
                if b == 0:
                    pe.wait_ge(s_rt, 2)
                for j in range(CH):
                    c = slice((b * CH + j) * P, (b * CH + j + 1) * P)
                    last = product(misc[:, j * E:(j + 1) * E], xT_hi[:, c], xT_lo[:, c], rt_hi[:, :], rt_lo[:, :],
                                   True, True)
                last.then_inc(s_logit, 1)

            def dense_transpose(first):
                pe.wait_ge(s_dense, 1 if first else 2)
                for k in range(1 if first else B - 1):
                    last = nc.tensor.transpose(misc[0:E * CH, k * P:(k + 1) * P],
                                               dense[:, k, :, :].rearrange("p e j -> p (e j)"), ident[:, :])
                last.then_inc(s_dT, 1)

            def bias_products():
                pe.wait_ge(s_const, 16 * N_CONST)
                pe.wait_ge(s_nb, 1)
                nc.tensor.matmul(bias_ps[0:1, 0:2 * D], nb_col, wqkv_raw[:, 0:2 * D], start=True, stop=True)
                nc.tensor.matmul(bias_ps[:, 2 * D:3 * D], nb_bc[:, :], wqkv_raw[:, D:2 * D], start=True, stop=True)
                nc.tensor.matmul(bias_ps[:, 3 * D:4 * D], wqkv_raw[:, 2 * D:3 * D], nb_bc[:, :], start=True,
                                 stop=True).then_inc(s_bias, 1)

            def att_gram(t):
                pe.wait_ge(s_z, 2 * t + 2)
                for j in range(CH):
                    last = nc.tensor.matmul(misc[:, 0:D + 1], z[:, j, 0:D], z[:, j, 0:D + 1], start=(j == 0),
                                            stop=(j == CH - 1))
                last.then_inc(s_G, 1)

            def att_keys(t):
                pe.wait_ge(s_Gc, t + 1)
                nc.tensor.matmul(misc[:, 0:D], mat_a[:, 0:D], wqkT[:, D:2 * D], start=True, stop=True)
                nc.tensor.matmul(misc[0:1, D:2 * D], mat_a[:, D:D + 1], wqkT[:, D:2 * D], start=True,
                                 stop=True).then_inc(s_X, 1)

            def att_scores(t):
                pe.wait_ge(s_Xc, 2 * t + 2)
                nc.tensor.matmul(misc[:, 0:D], wqkT[:, 0:D], mat_b, start=True, stop=False)
                nc.tensor.matmul(misc[:, 0:D], bq_row, r_row[0:1, :], start=False,
                                 stop=True).then_inc(s_S, 1)

            def att_mix(t):
                pe.wait_ge(s_w, t + 1)
                nc.tensor.matmul(misc[:, 0:D], mat_a[:, 0:D], proj_sb[:, :], start=True, stop=True).then_inc(s_M, 1)

            def att_fold(t):
                pe.wait_ge(s_Mc, t + 1)
                nc.tensor.matmul(misc[:, 0:D], wv_n[:, :], mat_b, start=True, stop=True)
                nc.tensor.matmul(misc[:, D:2 * D], bv_bc[:, :], mat_b, start=True, stop=True).then_inc(s_P, 1)

            def att_out(t):
                pe.wait_ge(s_Pc, t + 1)
                pe.wait_ge(s_obias, t + 1)
                pe.wait_ge(s_xcur, t + 1)
                for j in range(CH):
                    last = nc.tensor.matmul(misc[:, j * D:(j + 1) * D], x_cur[:, j * P:(j + 1) * P], mat_a[:, 0:D],
                                            start=True, stop=True)
                last.then_inc(s_U, 1)

            def attention(t, n, n0):
                if n == n0:
                    att_gram(t)
                if n == n0 + 2:
                    att_keys(t)
                if n == n0 + 4:
                    att_scores(t)
                if n == n0 + 9:
                    att_mix(t)
                if n == n0 + 11:
                    att_fold(t)
                if n == n0 + 13:
                    att_out(t)

            def final_transpose(t1):
                pe.wait_ge(s_y, t1)
                pe.wait_ge(s_attn, t1)
                for j in range(CH):
                    last = nc.tensor.transpose(misc[:, j * P:(j + 1) * P], yT[:, j * P:(j + 1) * P], ident[:, :])
                last.then_inc(s_yT, 1)

            transpose_x(0)
            router(0)
            bias_products()
            for n in range(NB):
                if n == U_RING - 1:
                    pe.wait_ge(s_attw, 5)
                gate_up(0, n, True)
                if n >= LAG:
                    down(0, n - LAG, True)
                if n == 0:
                    pe.wait_ge(s_lcopy, 1)
                    dense_transpose(True)
                if n == 3:
                    pe.wait_ge(s_dTcopy, 1)
                if n in (8, 13):
                    pe.wait_ge(s_lcopy, n // 5 + 1)
                if n in (3, 8, 13):
                    transpose_x(n // 5 + 1)
                if n in (6, 11, 16):
                    router(n // 5)
                if n == 25:
                    pe.wait_ge(s_lcopy, B)
                    dense_transpose(False)
                if n == ATT0:
                    pe.wait_ge(s_dTcopy, 2)
                attention(0, n, ATT0)
            with pe.Fori(1, B) as t:
                for n in range(NB):
                    gate_up(t, n, False)
                    if n < LAG:
                        down(t - 1, NB + n - LAG, False)
                    else:
                        down(t, n - LAG, False)
                    if n == LAG + 1:
                        final_transpose(t)
                    if n == ATT:
                        pe.wait_ge(s_comb, t)
                    attention(t, n, ATT)
            for m in range(NB - LAG, NB):
                down(B - 1, m, False)
            final_transpose(B)

        @block.scalar
        def _(act):
            def split_hi(c):
                act.wait_ge(s_wload[c % STAGES], 16 * (c // STAGES + 1))
                nc.scalar.copy(w_hi_v[:, c * CW:(c + 1) * CW], stage[:, c % STAGES, :]).then_inc(s_whi, 1)

            def silu(t, n, first):
                dt, m = prev(n, S_RING)
                if not (first and dt < 0):
                    act.wait_ge(s_h, t * NB + (dt * NB + m + 1))
                act.wait_ge(s_gate, t * NB + n + 1)
                nc.scalar.activation(s_buf[:, n % S_RING, :], gate_ps[n % G_RING], ACT.Silu).then_inc(s_silu, 1)

            def round_h(t, m, first):
                dt, k = prev(m, H_RING)
                if not (first and dt < 0):
                    act.wait_ge(s_down, t * NB + (dt * NB + k + 1))
                act.wait_ge(s_h, t * NB + m + 1)
                nc.scalar.copy(h_hi[:, m % H_RING, :], up_ps[m % U_RING]).then_inc(s_hhi, 1)

            def round_x(b):
                act.wait_ge(s_xpose, b + 1)
                nc.scalar.copy(xT_hi[:, b * L:(b + 1) * L], misc).then_inc(s_xhi, 1)

            def router_exp(first):
                act.wait_ge(s_lmax, 1 if first else 2)
                k = CH if first else NR
                nc.scalar.activation(ex[:, 0:k, :], ex[:, 0:k, :], ACT.Exp).then_inc(s_lexp, 1)

            def store_dense(first):
                act.wait_ge(s_dTcopy, 1 if first else 2)
                lo, hi = (0, 1) if first else (1, B)
                dst = dense_dram.rearrange("(b e) (j p) -> (e j) b p", b=B, j=CH)[:, lo:hi, :]
                act.dma_start(dst, denseT[:, 0:(hi - lo) * P].rearrange("q (b p) -> q b p", p=P)).then_inc(s_dram, 16)

            def copy_logits(b):
                k = max(b - 1, 0) * CH
                if b == 1:
                    act.wait_ge(s_dram, 16)
                act.wait_ge(s_logit, b + 1)
                nc.scalar.copy(lg[:, k:k + CH, :], misc[:, 0:CH * E].rearrange("p (j e) -> p j e", e=E)
                               ).then_inc(s_lcopy, 1)

            def copy_denseT(first):
                k = 1 if first else B - 1
                act.wait_ge(s_dT, 1 if first else 2)
                nc.scalar.copy(denseT[:, 0:k * P], misc[0:E * CH, 0:k * P]).then_inc(s_dTcopy, 1)

            def att_copy_gram(t):
                act.wait_ge(s_G, t + 1)
                nc.scalar.copy(mat_a, misc[:, 0:D + 1]).then_inc(s_Gc, 1)

            def att_copy_mix(t):
                act.wait_ge(s_M, t + 1)
                nc.scalar.copy(mat_b, misc[:, 0:D]).then_inc(s_Mc, 1)

            def att_copy_fold(t):
                act.wait_ge(s_obias, t + 1)
                nc.scalar.copy(mat_a[:, 0:D], misc[:, 0:D]).then_inc(s_Pc, 1)

            def att_exp(t):
                act.wait_ge(s_smax, t + 1)
                nc.scalar.activation(mat_a[:, 0:D], misc[:, 0:D], ACT.Exp, bias=sm[:, 1:2], scale=SCALE,
                                     accum_out=sm[:, 2:3]).then_inc(s_exp, 1)

            def ffn_silu(t1):
                act.wait_ge(s_down, t1 * NB)
                nc.scalar.activation(yT, ffn_ps, ACT.Silu).then_inc(s_y, 1)

            def load_again(t):
                act.dma_start(x_again, x_v[bass.ds(t, 1)].rearrange("b p j d -> (b p) j d")).then_inc(s_xagain, 16)

            def store(t):
                act.wait_ge(s_res, t + 1)
                act.dma_start(out_v[bass.ds(t, 1)].rearrange("b p j d -> (b p) j d"), o_sb).then_inc(s_out, 16)

            def attention(t, n, n0):
                if n == n0 + 1:
                    att_copy_gram(t)
                if n == n0 + 6:
                    att_exp(t)
                if n == n0 + 10:
                    att_copy_mix(t)
                if n == n0 + 12:
                    att_copy_fold(t)

            act.dma_start(rt_raw[:, :], routerT).then_inc(s_rtc, 16)
            act.dma_start(col_sb[:, :], columns).then_inc(s_const, 16)
            act.dma_start(row_sb[:, :], rows.broadcast_to([P, rows.shape[1]])).then_inc(s_const, 16)
            nc.scalar.preload_act_table(ACT.Exp)
            split_hi(0)
            round_x(0)
            split_hi(1)
            copy_logits(0)
            split_hi(2)
            router_exp(True)
            silu(0, 0, True)
            copy_denseT(True)
            store_dense(True)
            split_hi(3)
            split_hi(4)
            for n in range(NB):
                if n > 0:
                    silu(0, n, True)
                c = n // CHUNK + AHEAD - 1
                if n % CHUNK == 0 and AHEAD <= c < NCHUNK:
                    split_hi(c)
                if n >= ROUND_LAG:
                    round_h(0, n - ROUND_LAG, True)
                if n in (4, 9, 14):
                    round_x(n // 5 + 1)
                if n in (7, 12, 17):
                    copy_logits(n // 5)
                if n == 22:
                    router_exp(False)
                if n == 26:
                    copy_denseT(False)
                if n == 27:
                    store_dense(False)
                attention(0, n, ATT0)
            wait_split(act, NCHUNK - 1)
            wait_split(act, NCHUNK - 2)
            wait_split(act, NCHUNK - 3)
            load_again(0)
            with act.Fori(1, B) as t:
                for n in range(NB):
                    if n == LAG:
                        ffn_silu(t)
                    silu(t, n, False)
                    if n < ROUND_LAG:
                        round_h(t - 1, NB + n - ROUND_LAG, False)
                    else:
                        round_h(t, n - ROUND_LAG, False)
                    attention(t, n, ATT)
                    if n == LAG + 4:
                        store(t - 1)
                    if n == LAG + 9:
                        act.wait_ge(s_out, 16 * t)
                        load_again(t)
            for m in range(NB - ROUND_LAG, NB):
                round_h(B - 1, m, False)
            ffn_silu(B)
            store(B - 1)
            act.wait_ge(s_out, 16 * B)

        @block.gpsimd
        def _(pool):
            count = [0]

            def step(ins):
                count[0] += 1
                ins.then_inc(s_pool, 1)
                pool.wait_ge(s_pool, count[0])

            def weigh(t, n, first):
                q = pattern_of[n]
                if n == 0 or pattern_of[n - 1] != q:
                    all_loads = loads(len(patterns) - SLOTS + q % SLOTS)
                    pool.wait_ge(s_route[q % SLOTS], t * all_loads + loads(q))
                pool.wait_ge(s_silu, t * NB + n + 1)
                s = s_buf[:, n % S_RING, :]
                nc.gpsimd.tensor_tensor(s, s, route[:, q % SLOTS, :], ALU.mult).then_inc(s_weighted, 1)

            def inverse_root(b):
                c = slice(b * CH, (b + 1) * CH)
                pool.wait_ge(s_var, b + 1)
                nc.gpsimd.tensor_tensor(rstd[:, c], ve[:, c], mhalf[:, c], ALU.pow).then_inc(s_rstd, 1)

            def second_root(b0, b1):
                c = slice(b0 * CH, b1 * CH)
                pool.wait_ge(s_rstd, b1)
                step(nc.gpsimd.tensor_tensor(r2[:, c], mv[:, c, 1], rstd[:, c], ALU.mult))
                step(nc.gpsimd.tensor_tensor(r2[:, c], r2[:, c], rstd[:, c], ALU.mult))
                step(nc.gpsimd.tensor_scalar(r2[:, c], r2[:, c], LN_EPS, None, ALU.add))
                nc.gpsimd.tensor_tensor(r2[:, c], r2[:, c], mhalf[:, c], ALU.pow).then_inc(s_r2, 1)

            step(nc.gpsimd.memset(ident[:, :], 0.0))
            nc.gpsimd.affine_select(out=ident[:, :], in_=ident[:, :], compare_op=ALU.not_equal, fill=1.0, base=0,
                                    pattern=[[-1, P]], channel_multiplier=1).then_inc(s_ident, 1)
            step(nc.gpsimd.memset(mhalf[:, :], -0.5))
            inverse_root(0)
            inverse_root(1)
            split_lo(pool, 1)
            pool.wait_ge(s_const, 16 * N_CONST)
            nc.gpsimd.tensor_tensor(wv_n, wv_n, nw_bc, ALU.mult).then_inc(s_attw, 1)
            inverse_root(2)
            second_root(0, 3)
            inverse_root(3)
            for n in range(NB):
                c = n // CHUNK + AHEAD - 1
                weigh(0, n, True)
                if n % CHUNK == 0 and AHEAD - 1 <= c < NCHUNK and by_pool(c):
                    split_lo(pool, c)
                if n == 3:
                    second_root(3, 4)
            with pool.Fori(1, B) as t:
                for n in range(NB):
                    weigh(t, n, False)

        @block.vector
        def _(dve):
            count = [0]

            def step(ins):
                count[0] += 1
                ins.then_inc(s_dve, 1)
                dve.wait_ge(s_dve, count[0])

            def ln_stats(b):
                dve.wait_ge(s_x[b], 16)
                for j in range(CH):
                    last = nc.vector.bn_stats(stats[:, j, :], xn[:, b * CH + j, :])
                step(last)
                for j in range(CH):
                    last = nc.vector.bn_aggr(mv[:, b * CH + j, :], stats[:, j, :])
                step(last)
                c = slice(b * CH, (b + 1) * CH)
                nc.vector.tensor_scalar(ve[:, c], mv[:, c, 1], LN_EPS, None, ALU.add).then_inc(s_var, 1)

            def ln_apply(b):
                dve.wait_ge(s_rstd, b + 1)
                for j in range(b * CH, (b + 1) * CH):
                    last = nc.vector.tensor_scalar(xn[:, j, :], xn[:, j, :], mv[:, j, 0:1], rstd[:, j:j + 1],
                                                   ALU.subtract, ALU.mult)
                last.then_inc(s_ln, 1)

            def split_x(b):
                dve.wait_ge(s_xhi, b + 1)
                c = slice(b * L, (b + 1) * L)
                nc.vector.tensor_tensor(xT_lo[:, c], misc, xT_hi[:, c].bitcast(F32), ALU.subtract).then_inc(s_xlo, 1)

            def pick_top(k0, k):
                for j in range(k0, k0 + k):
                    last = nc.vector.max(top8[:, j, :], lg[:, j, :])
                step(last)
                for j in range(k0, k0 + k):
                    last = nc.vector.match_replace(lr[:, j, :], top8[:, j, :], lg[:, j, :], NEG)
                step(last)

            def shift_logits(k):
                nc.vector.tensor_tensor(ex[:, 0:k, :], lg[:, 0:k, :], top8[:, 0:k, 0:1].broadcast_to([P, k, E]),
                                        ALU.subtract).then_inc(s_lmax, 1)

            def dense_weights(first):
                k = CH if first else NR
                step(nc.vector.tensor_tensor(lr[:, 0:k, :], lr[:, 0:k, :], lg[:, 0:k, :], ALU.not_equal))
                dve.wait_ge(s_lexp, 1 if first else 2)
                step(nc.vector.tensor_tensor(ex[:, 0:k, :], ex[:, 0:k, :], lr[:, 0:k, :], ALU.mult))
                step(nc.vector.tensor_reduce(rsum[:, 0:k], ex[:, 0:k, :], AX_X, ALU.add))
                step(nc.vector.reciprocal(rsum[:, NR:NR + k], rsum[:, 0:k]))
                for b in range(k // CH):
                    j = slice(b * CH, (b + 1) * CH)
                    last = nc.vector.tensor_tensor(
                        dense[:, b, :, :].rearrange("p e j -> p j e"), ex[:, j, :],
                        rsum[:, NR + b * CH:NR + (b + 1) * CH].unsqueeze(2).broadcast_to([P, CH, E]), ALU.mult)
                last.then_inc(s_dense, 1)

            def hidden(t, n):
                dve.wait_ge(s_up, t * NB + n + 1)
                dve.wait_ge(s_weighted, t * NB + n + 1)
                nc.vector.tensor_tensor(up_ps[n % U_RING], s_buf[:, n % S_RING, :], up_ps[n % U_RING],
                                        ALU.mult).then_inc(s_h, 1)

            def split_h(t, m):
                dve.wait_ge(s_hhi, t * NB + m + 1)
                nc.vector.tensor_tensor(h_lo[:, m % H_RING, :], up_ps[m % U_RING], h_hi[:, m % H_RING, :].bitcast(F32),
                                        ALU.subtract).then_inc(s_hlo, 1)

            def spread_norm_b():
                dve.wait_ge(s_const, 16 * N_CONST)
                step(nc.vector.memset(nb_bc[:, :], 1.0))
                nc.vector.tensor_scalar(nb_bc[:, :], nb_bc[:, :], nb_col, None, ALU.mult).then_inc(s_nb, 1)

            def fold_norm():
                dve.wait_ge(s_bias, 1)
                nc.vector.tensor_scalar(wqkT, wqkT, nw_col, None, ALU.mult).then_inc(s_attw, 1)
                step(nc.vector.tensor_tensor(bkL_row[:, :], bias_ps[0:1, D:2 * D], bk_bc[0:1, :], ALU.add))
                step(nc.vector.tensor_scalar(bkL_row[:, :], bkL_row[:, :], float(L), None, ALU.mult))
                nc.vector.tensor_tensor(bq_row, bias_ps[0:1, 0:D], bq_row, ALU.add).then_inc(s_attw, 1)
                nc.vector.tensor_tensor(bk_bc, bias_ps[:, 2 * D:3 * D], bk_bc, ALU.add).then_inc(s_attw, 1)
                nc.vector.tensor_scalar(bv_bc[:, :], bias_ps[:, 3 * D:4 * D], bv_col, None, ALU.add).then_inc(s_attw, 1)

            def att_copy_keys(t):
                dve.wait_ge(s_X, t + 1)
                nc.vector.scalar_tensor_tensor(out=mat_b, in0=bk_bc, scalar=mat_a[:, D:D + 1],
                                               in1=misc[:, 0:D], op0=ALU.mult, op1=ALU.add).then_inc(s_Xc, 1)
                nc.vector.tensor_tensor(r_row[:, :], misc[0:1, D:2 * D], bkL_row[:, :], ALU.add).then_inc(s_Xc, 1)

            def att_max(t, t2):
                dve.wait_ge(s_S, t + 1)
                nc.vector.tensor_reduce(sm[:, 0:1], misc[:, 0:D], AX_X, ALU.max).then_inc(s_dve, 1)
                dve.wait_ge(s_dve, t2 + 2)
                nc.vector.tensor_scalar(sm[:, 1:2], sm[:, 0:1], -SCALE, None, ALU.mult).then_inc(s_smax, 1)

            def att_normalise(t, t2):
                dve.wait_ge(s_exp, t + 1)
                nc.vector.reciprocal(sm[:, 3:4], sm[:, 2:3]).then_inc(s_dve, 1)
                dve.wait_ge(s_dve, t2 + 3)
                nc.vector.tensor_scalar(mat_a[:, 0:D], mat_a[:, 0:D], sm[:, 3:4], None, ALU.mult).then_inc(s_w, 1)

            def att_bias(t):
                dve.wait_ge(s_P, t + 1)
                nc.vector.tensor_tensor(out_bias, misc[:, D:2 * D], pb_bc, ALU.add).then_inc(s_obias, 1)
                v = xn[:, bass.ds(t * CH, CH), :]
                dve.wait_ge(s_obias, t + 1)
                nc.vector.tensor_tensor(v, v, out_bias.unsqueeze(1).broadcast_to([P, CH, D]),
                                        ALU.add).then_inc(s_base, 1)

            def att_finish(t):
                dve.wait_ge(s_U, t + 1)
                dve.wait_ge(s_base, t + 1)
                for j in range(CH):
                    v = xn[:, bass.ds(t * CH + j, 1), :].rearrange("p o d -> p (o d)")
                    last = nc.vector.scalar_tensor_tensor(out=v, in0=misc[:, j * D:(j + 1) * D],
                                                          scalar=r2_cur[:, j:j + 1], in1=v, op0=ALU.mult, op1=ALU.add)
                last.then_inc(s_attn, 1)

            def make_z(t, t2):
                nc.vector.tensor_copy(r2_cur[:, :], r2[:, bass.ds(t * CH, CH)]).then_inc(s_dve, 1)
                nc.vector.memset(z[:, :, D:D + 1], 1.0).then_inc(s_z, 1)
                dve.wait_ge(s_dve, t2 + 1)
                nc.vector.tensor_tensor(z[:, :, 0:D], xn[:, bass.ds(t * CH, CH), :],
                                        r2_cur[:, :].unsqueeze(2).broadcast_to([P, CH, D]), ALU.mult).then_inc(s_z, 1)

            def make_x_cur(t):
                nc.vector.tensor_tensor(x_cur, tile_cols(xT_hi, t).bitcast(F32), tile_cols(xT_lo, t).bitcast(F32),
                                        ALU.add).then_inc(s_xcur, 1)

            def attention(t, t3, n, n0):
                if n == n0 - 2:
                    make_z(t, t3)
                if n == n0 + 1:
                    dve.wait_ge(s_G, t + 1)
                    make_x_cur(t)
                if n == n0 + 2:
                    att_copy_keys(t)
                if n == n0 + 4:
                    att_max(t, t3)
                if n == n0 + 7:
                    att_normalise(t, t3)
                if n == n0 + 11:
                    att_bias(t)
                if n == n0 + 13:
                    att_finish(t)

            def combine(t):
                dve.wait_ge(s_yT, t + 1)
                dve.wait_ge(s_xagain, 16 * t + 16)
                nc.vector.tensor_tensor(o_sb, misc.rearrange("p (j d) -> p j d", j=CH),
                                        xn[:, bass.ds(t * CH, CH), :], ALU.mult).then_inc(s_comb, 1)
                dve.wait_ge(s_comb, t + 1)
                nc.vector.tensor_tensor(o_sb, o_sb, x_again, ALU.add).then_inc(s_res, 1)

            dve.wait_ge(s_rtc, 16)
            nc.vector.tensor_copy(rt_hi[:, :], rt_raw[:, :]).then_inc(s_rt, 1)
            dve.wait_ge(s_rt, 1)
            nc.vector.tensor_tensor(rt_lo[:, :], rt_raw[:, :], rt_hi[:, :].bitcast(F32),
                                    ALU.subtract).then_inc(s_rt, 1)
            ln_stats(0)
            ln_apply(0)
            split_lo(dve, 0)
            spread_norm_b()
            split_x(0)
            ln_stats(1)
            ln_apply(1)
            ln_stats(2)
            dve.wait_ge(s_lcopy, 1)
            pick_top(0, CH)
            shift_logits(CH)
            dense_weights(True)
            fold_norm()
            split_lo(dve, 2)
            ln_stats(3)
            ln_apply(2)
            split_lo(dve, 3)
            ln_apply(3)
            for n in range(NB):
                c = n // CHUNK + AHEAD - 1
                if n >= ROUND_LAG:
                    split_h(0, n - ROUND_LAG)
                hidden(0, n)
                if n % CHUNK == 0 and AHEAD <= c < NCHUNK and not by_pool(c):
                    split_lo(dve, c)
                if n in (4, 9, 14):
                    split_x(n // 5 + 1)
                if n == 18:
                    dve.wait_ge(s_lcopy, B)
                if n in (18, 19, 20):
                    pick_top((n - 18) * CH, CH)
                if n == 20:
                    shift_logits(NR)
                if n == 23:
                    dense_weights(False)
                if n == ATT0 - 2:
                    dve.wait_ge(s_r2, 2)
                    dve.wait_ge(s_dram, 32)
                attention(0, count[0], n, ATT0)
            base = count[0]
            with dve.Fori(1, B) as t:
                for n in range(NB):
                    if n < ROUND_LAG:
                        split_h(t - 1, NB + n - ROUND_LAG)
                    else:
                        split_h(t, n - ROUND_LAG)
                    hidden(t, n)
                    if n == LAG + 1:
                        combine(t - 1)
                    attention(t, t * 3 + base, n, ATT)
            for m in range(NB - ROUND_LAG, NB):
                split_h(B - 1, m)
            combine(B - 1)


def kernel(L0_attn_x, L0_attn_norm_w, L0_attn_norm_b, L0_attn_qkv_w, L0_attn_qkv_b, L0_attn_proj_w, L0_attn_proj_b,
           L0_ffn_router_w, L0_ffn_gate_w, L0_ffn_up_w, L0_ffn_down_w):
    import numpy as np
    import concourse.bacc as bacc
    from concourse.bass_utils import run_bass_kernel_spmd

    x = np.asarray(L0_attn_x)
    B, L, D = x.shape
    qkv_w = np.asarray(L0_attn_qkv_w)
    E, F, H = L0_ffn_gate_w.shape
    NB = E * F // P
    gate = np.asarray(L0_ffn_gate_w).reshape(NB, P, H).transpose(2, 0, 1)
    up = np.asarray(L0_ffn_up_w).reshape(NB, P, H).transpose(2, 0, 1)
    down = np.asarray(L0_ffn_down_w).transpose(0, 2, 1).reshape(NB, P, H).transpose(1, 0, 2)
    norm_w, norm_b, qkv_b, proj_b = (np.asarray(v) for v in (L0_attn_norm_w, L0_attn_norm_b, L0_attn_qkv_b,
                                                             L0_attn_proj_b))
    arrays = {
        "x": x,
        "columns": np.concatenate([qkv_w.T, qkv_w[2 * D:], np.asarray(L0_attn_proj_w).T, norm_w[:, None],
                                   norm_b[:, None], qkv_b[2 * D:, None]], axis=1),
        "rows": np.concatenate([norm_w, qkv_b, proj_b])[None, :],
        "routerT": np.asarray(L0_ffn_router_w).T, "w_all": np.stack([gate, up, down], axis=2),
    }
    arrays = {k: np.ascontiguousarray(v) for k, v in arrays.items()}
    nc = bacc.Bacc("TRN2", target_bir_lowering=False, num_devices=1)
    args = [nc.dram_tensor(k, v.shape, F32, kind="ExternalInput").ap() for k, v in arrays.items()]
    dense = nc.dram_tensor("dense_w", (B * E, L), F32, kind="Internal").ap()
    out = nc.dram_tensor("out", (B, L, D), F32, kind="ExternalOutput").ap()
    gated_block(nc, *args, dense, out)
    r = run_bass_kernel_spmd(nc, [arrays], core_ids=[0])
    return r.results[0]["out"]
```

```python
from contextlib import ExitStack

import concourse.bass as bass
from concourse import mybir

F32 = mybir.dt.float32
F32R = mybir.dt.float32r
ALU = mybir.AluOpType
ACT = mybir.ActivationFunctionType
AX_X = mybir.AxisListType.X

P = 128
LN_EPS = 1e-5
TOP_K = 8
LAG = 4
G_RING = 2
U_RING = 4
S_RING = 3
H_RING = 4
ROUND_LAG = 2
CHUNK = 2
STAGES = 3
AHEAD = 4
WARM_UP, WARM_KEEP = 14, 6
NEG = -3.4028235e38


def block_pattern(n, per_expert):
    out, f = [], n * P
    while f < (n + 1) * P:
        e = f // per_expert
        end = min((e + 1) * per_expert, (n + 1) * P)
        out.append((e, f - n * P, end - n * P))
        f = end
    return out


def gated_block(nc, x, columns, rows, routerT, w_all, dense_dram, out):
    B, L, D = x.shape
    E = routerT.shape[1]
    NB = w_all.shape[1]
    FE = NB * P // E
    CH = L // P
    NCHUNK = NB // CHUNK
    SCALE = float(L) ** -0.5
    assert D == P and L == 512 and NB % CHUNK == 0 and E * CH <= P

    patterns, pattern_of = [], []
    for n in range(NB):
        cut = block_pattern(n, FE)
        if not patterns or patterns[-1] != cut:
            patterns.append(cut)
        pattern_of.append(len(patterns) - 1)
    last_block = [max(n for n in range(NB) if pattern_of[n] == q) for q in range(len(patterns))]
    SLOTS = 4
    assert len(patterns) % SLOTS == 0

    def loads(q):
        return 16 * sum(len(patterns[k]) for k in range(q % SLOTS, q + 1, SLOTS))

    def prev(n, depth):
        if n >= depth:
            return 0, n - depth
        return -1, max(m for m in range(NB) if m % depth == n % depth)

    with ExitStack() as ctx:
        def sb(name, shape, dt=F32):
            return ctx.enter_context(nc.sbuf_tensor(name, shape, dt))

        def sem(name):
            return ctx.enter_context(nc.semaphore(name))

        psum = ctx.enter_context(nc.psum_tensor("psum", [P, 8, 512], F32))
        gate_ps = [psum[:, r, :] for r in range(G_RING)]
        up_ps = [psum[:, G_RING + r, :] for r in range(U_RING)]
        ffn_ps = psum[:, 6, :]
        misc = psum[:, 7, :]
        end_ps = [misc, gate_ps[0]]
        bias_ps = up_ps[U_RING - 1]

        w_hi = sb("w_hi", [P, NB, 3, P], F32R)
        w_lo = sb("w_lo", [P, NB, 3, P], F32R)
        xT_hi = sb("xT_hi", [P, B * L], F32R)
        xT_lo = sb("xT_lo", [P, B * L], F32R)
        xn = sb("xn", [P, B * CH, D])
        route = sb("route", [P, SLOTS, L])
        s_buf = sb("s_buf", [P, S_RING, L])
        h_hi = sb("h_hi", [P, H_RING, L], F32R)
        h_lo = sb("h_lo", [P, H_RING, L], F32R)
        stage = sb("stage", [P, STAGES, CHUNK * 3 * P])
        tail = stage[:, :, :].rearrange("p s n -> p (s n)")
        assert STAGES * CHUNK * 3 * P >= 3 * L
        yT = tail[:, 0:L]
        o_sb = tail[:, L:2 * L].rearrange("p (j d) -> p j d", j=CH)
        x_again = tail[:, 2 * L:3 * L].rearrange("p (j d) -> p j d", j=CH)

        col_sb = sb("col_sb", [P, columns.shape[1]])
        wqkv_raw = col_sb[:, 0:3 * D]
        wqkT = col_sb[:, 0:2 * D]
        wv_n = col_sb[:, 3 * D:4 * D]
        proj_sb = col_sb[:, 4 * D:5 * D]
        nw_col, nb_col, bv_col = (col_sb[:, 5 * D + i:5 * D + i + 1] for i in range(3))
        row_sb = sb("row_sb", [P, rows.shape[1]])
        nw_bc, bk_bc, pb_bc = row_sb[:, 0:D], row_sb[:, 2 * D:3 * D], row_sb[:, 4 * D:5 * D]
        bq_row = row_sb[0:1, D:2 * D]
        nb_bc = sb("nb_bc", [P, P])
        bv_bc = sb("bv_bc", [P, P])
        ident = sb("ident", [P, P])
        bkL_row = sb("bkL_row", [1, D])
        r_row = sb("r_row", [1, D])
        rt_raw = sb("rt_raw", [P, E])
        rt_parts = sb("rt_parts", [P, 2 * E], F32R)
        rt_hi, rt_lo = rt_parts[:, 0:E], rt_parts[:, E:2 * E]
        stats = sb("stats", [P, CH, 6])
        mv = sb("mv", [P, B * CH, 2])
        ve = sb("ve", [P, B * CH])
        mhalf = sb("mhalf", [P, B * CH])
        rstd = sb("rstd", [P, B * CH])
        r2 = sb("r2", [P, B * CH])
        r2_cur = sb("r2_cur", [P, CH])
        sm = sb("sm", [P, 4])
        rsum = sb("rsum", [P, 2 * 3 * CH])

        scratch = sb("scratch", [P, 4 * 129 + 2 * 130 + P])
        z = scratch[:, 0:CH * 129].rearrange("p (j d) -> p j d", j=CH)
        x_cur = scratch[:, 0:L]
        mat_a = scratch[:, 516:516 + 129]
        mat_b = scratch[:, 646:646 + D]
        out_bias = scratch[:, 776:776 + D]
        NR = 3 * CH
        lg = scratch[:, 0:NR * E].rearrange("p (j e) -> p j e", e=E)
        lr = scratch[:, NR * E:2 * NR * E].rearrange("p (j e) -> p j e", e=E)
        ex = scratch[:, 2 * NR * E:3 * NR * E].rearrange("p (j e) -> p j e", e=E)
        dense = scratch[:, 3 * NR * E:4 * NR * E].rearrange("p (b e j) -> p b e j", e=E, j=CH)
        top8 = scratch[:, 4 * NR * E:4 * NR * E + NR * 8].rearrange("p (j k) -> p j k", k=8)
        denseT = scratch[0:E * CH, 516:516 + 3 * P]

        s_x = [sem(f"s_x{b}") for b in range(B)]
        s_const = sem("s_const")
        s_rtc = sem("s_rtc")
        s_wload = [sem(f"s_wload{i}") for i in range(STAGES)]
        s_whi, s_wlo_dve, s_wlo_pool = sem("s_whi"), sem("s_wlo_dve"), sem("s_wlo_pool")
        s_pattern = sem("s_pattern")
        s_route = [sem(f"s_route{i}") for i in range(SLOTS)]
        s_xagain, s_out = sem("s_xagain"), sem("s_out")
        s_ident = sem("s_ident")
        s_dve = sem("s_dve")
        s_pool = sem("s_pool")
        s_var, s_rstd, s_ln, s_r2 = sem("s_var"), sem("s_rstd"), sem("s_ln"), sem("s_r2")
        s_xpose, s_xhi, s_xlo = sem("s_xpose"), sem("s_xhi"), sem("s_xlo")
        s_rt = sem("s_rt")
        s_logit, s_lsum, s_logits = sem("s_logit"), sem("s_lsum"), sem("s_logits")
        s_lmax, s_lexp = sem("s_lmax"), sem("s_lexp")
        s_dense, s_dT, s_dTcopy, s_dram = sem("s_dense"), sem("s_dT"), sem("s_dTcopy"), sem("s_dram")
        s_gate, s_up, s_down = sem("s_gate"), sem("s_up"), sem("s_down")
        s_silu, s_weighted, s_h, s_hhi, s_hlo = (sem("s_silu"), sem("s_weighted"), sem("s_h"), sem("s_hhi"),
                                                 sem("s_hlo"))
        s_nb, s_bias, s_attw = sem("s_nb"), sem("s_bias"), sem("s_attw")
        s_z, s_G, s_Gc, s_X, s_Xc, s_S = sem("s_z"), sem("s_G"), sem("s_Gc"), sem("s_X"), sem("s_Xc"), sem("s_S")
        s_smax, s_exp, s_w, s_M, s_Mc, s_P, s_Pc = (sem("s_smax"), sem("s_exp"), sem("s_w"), sem("s_M"),
                                                    sem("s_Mc"), sem("s_P"), sem("s_Pc"))
        s_obias = sem("s_obias")
        s_xcur, s_biased, s_U, s_attn = sem("s_xcur"), sem("s_biased"), sem("s_U"), sem("s_attn")
        s_y, s_yT, s_comb, s_res = sem("s_y"), sem("s_yT"), sem("s_comb"), sem("s_res")
        N_CONST = 2
        STATS_AT = {10: 3}
        ROOT_AT = {7: 2, 12: 3}
        APPLY_AT = {9: 2, 14: 3}
        XPOSE_AT = {3: 1, 11: 2, 16: 3}
        ROUTER_AT = {6: 1, 14: 2, 19: 3}
        PICK_AT = {9: 1, 16: 2, 20: 3}
        ROOT2_AT = {10: 0, 16: 1, 20: 2, 24: 3}
        SHIFT, MARK, EXP, SUM, WEIGHTS, TO_T, OUT_T = 20, 21, 22, 24, 25, 27, 28
        ATT0, ATT = 30, 10
        assert B == 4 and STAGES <= B

        x_v = x.rearrange("b (p j) d -> b p j d", j=CH)
        out_v = out.rearrange("b (p j) d -> b p j d", j=CH)
        w_v = w_all.rearrange("p n k m -> p (n k m)")
        w_hi_v = w_hi[:, :, :, :].rearrange("p n k m -> p (n k m)")
        w_lo_v = w_lo[:, :, :, :].rearrange("p n k m -> p (n k m)")
        CW = CHUNK * 3 * P

        def by_pool(c):
            return c % 3 == 1

        def chunk_at(n):
            c = (n - 3) // CHUNK + AHEAD
            return c if (n - 3) % CHUNK == 0 and AHEAD <= c < NCHUNK else -1

        def wait_split(eng, c):
            own = by_pool(c)
            eng.wait_ge(s_wlo_pool if own else s_wlo_dve, sum(by_pool(k) == own for k in range(c + 1)))

        def split_lo(eng, c):
            eng.wait_ge(s_whi, c + 1)
            eng.tensor_tensor(w_lo_v[:, c * CW:(c + 1) * CW], stage[:, c % STAGES, :],
                              w_hi_v[:, c * CW:(c + 1) * CW].bitcast(F32), ALU.subtract
                              ).then_inc(s_wlo_pool if by_pool(c) else s_wlo_dve, 1)

        def half(k):
            return slice(k * L // 2, (k + 1) * L // 2)

        def tile_cols(buf, t):
            return buf[:, bass.ds(t * L, L)]

        def store_dense(eng, first):
            eng.wait_ge(s_dTcopy, 1 if first else 2)
            lo, hi = (0, 1) if first else (1, B)
            dst = dense_dram.rearrange("(b e) (j p) -> (e j) b p", b=B, j=CH)[:, lo:hi, :]
            eng.dma_start(dst, denseT[:, 0:(hi - lo) * P].rearrange("q (b p) -> q b p", p=P)).then_inc(s_dram, 16)

        block = ctx.enter_context(nc.Block())

        @block.sync
        def _(sp):
            def load_weights(c):
                if c >= STAGES:
                    wait_split(sp, c - STAGES)
                sp.dma_start(stage[:, c % STAGES, :], w_v[:, c * CW:(c + 1) * CW]).then_inc(s_wload[c % STAGES], 16)

            def load_pattern(t, q, first):
                slot = q % SLOTS
                if q == (1 if first else 0):
                    sp.wait_ge(s_dram, 16 if first else 32)
                if q >= SLOTS:
                    sp.wait_ge(s_weighted, t * NB + last_block[q - SLOTS] + 1)
                elif not first:
                    sp.wait_ge(s_weighted, t * NB + (last_block[q - SLOTS + len(patterns)] + 1 - NB))
                for e, a, b in patterns[q]:
                    src = dense_dram[bass.ds(t * E + e, 1), :].broadcast_to([b - a, L])
                    sp.dma_start(route[a:b, slot, :], src).then_inc(s_route[slot], 16)

            sp.dma_start(xn[:, 0:CH, :], x_v[0]).then_inc(s_x[0], 16)
            load_weights(0)
            for b in range(1, B):
                if b < STAGES:
                    load_weights(b)
                sp.dma_start(xn[:, b * CH:(b + 1) * CH, :], x_v[b]).then_inc(s_x[b], 16)
            for c in range(STAGES, AHEAD + 1):
                load_weights(c)
            store_dense(sp, True)
            load_pattern(0, 1, True)
            load_weights(AHEAD + 1)
            for q in range(2, SLOTS):
                load_pattern(0, q, True)
            for n in range(NB):
                if n % CHUNK == 0 and n // CHUNK + AHEAD + 2 < NCHUNK:
                    load_weights(n // CHUNK + AHEAD + 2)
                for q in range(SLOTS, len(patterns)):
                    if last_block[q - SLOTS] == n:
                        load_pattern(0, q, True)
            with sp.Fori(1, B) as t:
                for q in range(len(patterns)):
                    load_pattern(t, q, False)

        @block.tensor
        def _(pe):
            def product(dst, lhi, llo, rhi, rlo, start, stop):
                nc.tensor.matmul(dst, lhi, rhi, start=start, stop=False)
                nc.tensor.matmul(dst, lhi, rlo, start=False, stop=False)
                return nc.tensor.matmul(dst, llo, rhi, start=False, stop=stop)

            def first_pattern():
                pe.wait_ge(s_dTcopy, 1)
                for j in range(CH):
                    last = nc.tensor.matmul(misc[:, j * P:(j + 1) * P],
                                            ident[0:E * CH, j:j + 1].broadcast_to([E * CH, P]), denseT[:, 0:P],
                                            start=True, stop=True)
                last.then_inc(s_pattern, 1)

            def gate_up(t, n, first):
                if first and n % CHUNK == 0:
                    wait_split(pe, n // CHUNK)
                xh, xl = tile_cols(xT_hi, t), tile_cols(xT_lo, t)
                dt, m = prev(n, G_RING)
                if not (first and dt < 0):
                    pe.wait_ge(s_silu, t * NB + (dt * NB + m + 1))
                product(gate_ps[n % G_RING], w_hi[:, n, 0, :], w_lo[:, n, 0, :], xh, xl, True, True).then_inc(s_gate, 1)
                dt, m = prev(n, U_RING)
                if not (first and dt < 0):
                    pe.wait_ge(s_hlo, t * NB + (dt * NB + m + 1))
                product(up_ps[n % U_RING], w_hi[:, n, 1, :], w_lo[:, n, 1, :], xh, xl, True, True).then_inc(s_up, 1)

            def down(t, m, first):
                if m == 0 and not first:
                    pe.wait_ge(s_y, t)
                pe.wait_ge(s_hlo, t * NB + m + 1)
                product(ffn_ps, w_hi[:, m, 2, :], w_lo[:, m, 2, :], h_hi[:, m % H_RING, :], h_lo[:, m % H_RING, :],
                        m == 0, m == NB - 1).then_inc(s_down, 1)

            def keep_busy(k):
                for _ in range(k):
                    nc.tensor.matmul(bias_ps[:, 0:P], ident[:, :], ident[:, :], start=True, stop=True)

            def transpose_x(b):
                pe.wait_ge(s_ln, b + 1)
                for j in range(CH):
                    last = nc.tensor.transpose(misc[:, j * P:(j + 1) * P], xn[:, b * CH + j, :], ident[:, :])
                last.then_inc(s_xpose, 1)

            def router(b):
                pe.wait_ge(s_xlo, b + 1)
                if b == 0:
                    pe.wait_ge(s_rt, 2)
                for j in range(CH):
                    c = slice((b * CH + j) * P, (b * CH + j + 1) * P)
                    nc.tensor.matmul(misc[:, 2 * j * E:2 * (j + 1) * E], xT_hi[:, c], rt_parts[:, :], start=True,
                                     stop=False)
                    last = nc.tensor.matmul(misc[:, 2 * j * E:(2 * j + 1) * E], xT_lo[:, c], rt_hi, start=False,
                                            stop=True)
                last.then_inc(s_logit, 1)

            def dense_transpose(first):
                pe.wait_ge(s_dense, 1 if first else 2)
                for k in range(1 if first else B - 1):
                    last = nc.tensor.transpose(misc[0:E * CH, k * P:(k + 1) * P],
                                               dense[:, k, :, :].rearrange("p e j -> p (e j)"), ident[:, :])
                last.then_inc(s_dT, 1)

            def bias_products():
                pe.wait_ge(s_const, 16 * N_CONST)
                pe.wait_ge(s_nb, 1)
                nc.tensor.matmul(bias_ps[0:1, 0:2 * D], nb_col, wqkv_raw[:, 0:2 * D], start=True, stop=True)
                nc.tensor.matmul(bias_ps[:, 2 * D:3 * D], nb_bc[:, :], wqkv_raw[:, D:2 * D], start=True, stop=True)
                nc.tensor.matmul(bias_ps[:, 3 * D:4 * D], wqkv_raw[:, 2 * D:3 * D], nb_bc[:, :], start=True,
                                 stop=True).then_inc(s_bias, 1)

            def att_gram(t):
                pe.wait_ge(s_z, 2 * t + 2)
                for j in range(CH):
                    last = nc.tensor.matmul(misc[:, 0:D + 1], z[:, j, 0:D], z[:, j, 0:D + 1], start=(j == 0),
                                            stop=(j == CH - 1))
                last.then_inc(s_G, 1)

            def att_keys(t):
                pe.wait_ge(s_Gc, t + 1)
                nc.tensor.matmul(misc[:, 0:D], mat_a[:, 0:D], wqkT[:, D:2 * D], start=True, stop=True)
                nc.tensor.matmul(misc[0:1, D:2 * D], mat_a[:, D:D + 1], wqkT[:, D:2 * D], start=True,
                                 stop=True).then_inc(s_X, 1)

            def att_scores(t):
                pe.wait_ge(s_Xc, 2 * t + 2)
                nc.tensor.matmul(misc[:, 0:D], wqkT[:, 0:D], mat_b, start=True, stop=False)
                nc.tensor.matmul(misc[:, 0:D], bq_row, r_row[0:1, :], start=False,
                                 stop=True).then_inc(s_S, 1)

            def att_mix(t):
                pe.wait_ge(s_w, t + 1)
                nc.tensor.matmul(misc[:, 0:D], mat_a[:, 0:D], proj_sb[:, :], start=True, stop=True).then_inc(s_M, 1)

            def att_fold(t):
                pe.wait_ge(s_Mc, t + 1)
                nc.tensor.matmul(misc[:, 0:D], wv_n[:, :], mat_b, start=True, stop=True)
                nc.tensor.matmul(misc[:, D:2 * D], bv_bc[:, :], mat_b, start=True, stop=True).then_inc(s_P, 1)

            def att_out(t):
                pe.wait_ge(s_Pc, t + 1)
                pe.wait_ge(s_obias, t + 1)
                pe.wait_ge(s_xcur, t + 1)
                for j in range(CH):
                    last = nc.tensor.matmul(misc[:, j * D:(j + 1) * D], x_cur[:, j * P:(j + 1) * P], mat_a[:, 0:D],
                                            start=True, stop=True)
                last.then_inc(s_U, 1)

            def attention(t, n, n0):
                if n == n0:
                    att_gram(t)
                if n == n0 + 2:
                    att_keys(t)
                if n == n0 + 4:
                    att_scores(t)
                if n == n0 + 9:
                    att_mix(t)
                if n == n0 + 11:
                    att_fold(t)
                if n == n0 + 13:
                    att_out(t)

            def final_transpose(t1):
                pe.wait_ge(s_y, t1)
                pe.wait_ge(s_attn, t1)
                for j in range(CH):
                    last = nc.tensor.transpose(misc[:, j * P:(j + 1) * P], yT[:, j * P:(j + 1) * P], ident[:, :])
                last.then_inc(s_yT, 1)

            pe.wait_ge(s_ident, 1)
            keep_busy(WARM_UP)
            transpose_x(0)
            keep_busy(WARM_KEEP)
            router(0)
            for n in range(NB):
                if n == U_RING - 1:
                    pe.wait_ge(s_attw, 5)
                gate_up(0, n, True)
                if n >= LAG:
                    down(0, n - LAG, True)
                if n == 1:
                    bias_products()
                    pe.wait_ge(s_logits, 1)
                    dense_transpose(True)
                    first_pattern()
                if n == 3:
                    pe.wait_ge(s_route[0], 16)
                if n in XPOSE_AT:
                    if XPOSE_AT[n] > 1:
                        pe.wait_ge(s_logits, XPOSE_AT[n])
                    transpose_x(XPOSE_AT[n])
                if n in ROUTER_AT:
                    router(ROUTER_AT[n])
                if n == TO_T:
                    pe.wait_ge(s_logits, B)
                    dense_transpose(False)
                if n == ATT0:
                    pe.wait_ge(s_dTcopy, 2)
                attention(0, n, ATT0)
            with pe.Fori(1, B) as t:
                for n in range(NB):
                    gate_up(t, n, False)
                    if n < LAG:
                        down(t - 1, NB + n - LAG, False)
                    else:
                        down(t, n - LAG, False)
                    if n == LAG + 1:
                        final_transpose(t)
                    if n == ATT:
                        pe.wait_ge(s_comb, t)
                    attention(t, n, ATT)
            for m in range(NB - LAG, NB - 1):
                down(B - 1, m, False)
            m, slot = NB - 1, (NB - 1) % H_RING
            pe.wait_ge(s_hhi, B * NB)
            nc.tensor.matmul(ffn_ps, w_hi[:, m, 2, :], h_hi[:, slot, :], start=False, stop=False)
            nc.tensor.matmul(ffn_ps, w_lo[:, m, 2, :], h_hi[:, slot, :], start=False, stop=False)
            pe.wait_ge(s_hlo, B * NB)
            nc.tensor.matmul(ffn_ps, w_hi[:, m, 2, :], h_lo[:, slot, :], start=False, stop=True).then_inc(s_down, 1)
            pe.wait_ge(s_attn, B)
            for k in range(2):
                pe.wait_ge(s_y, B + k)
                for j in range(CH // 2):
                    last = nc.tensor.transpose(end_ps[k][:, j * P:(j + 1) * P], yT[:, half(k)][:, j * P:(j + 1) * P],
                                               ident[:, :])
                last.then_inc(s_yT, 1)

        @block.scalar
        def _(act):
            def split_hi(c):
                act.wait_ge(s_wload[c % STAGES], 16 * (c // STAGES + 1))
                nc.scalar.copy(w_hi_v[:, c * CW:(c + 1) * CW], stage[:, c % STAGES, :]).then_inc(s_whi, 1)

            def silu(t, n, first):
                dt, m = prev(n, S_RING)
                if not (first and dt < 0):
                    act.wait_ge(s_h, t * NB + (dt * NB + m + 1))
                act.wait_ge(s_gate, t * NB + n + 1)
                nc.scalar.activation(s_buf[:, n % S_RING, :], gate_ps[n % G_RING], ACT.Silu).then_inc(s_silu, 1)

            def round_h(t, m, first):
                dt, k = prev(m, H_RING)
                if not (first and dt < 0):
                    act.wait_ge(s_down, t * NB + (dt * NB + k + 1))
                act.wait_ge(s_h, t * NB + m + 1)
                nc.scalar.copy(h_hi[:, m % H_RING, :], up_ps[m % U_RING]).then_inc(s_hhi, 1)

            def round_x(b):
                act.wait_ge(s_xpose, b + 1)
                nc.scalar.copy(xT_hi[:, b * L:(b + 1) * L], misc).then_inc(s_xhi, 1)

            def router_exp(first):
                act.wait_ge(s_lmax, 1 if first else 2)
                k = CH if first else NR
                nc.scalar.activation(ex[:, 0:k, :], ex[:, 0:k, :], ACT.Exp).then_inc(s_lexp, 1)

            def copy_denseT(first):
                k = 1 if first else B - 1
                act.wait_ge(s_dT, 1 if first else 2)
                nc.scalar.copy(denseT[:, 0:k * P], misc[0:E * CH, 0:k * P]).then_inc(s_dTcopy, 1)

            def copy_pattern():
                act.wait_ge(s_pattern, 1)
                nc.scalar.copy(route[:, 0, :], misc).then_inc(s_route[0], 16)

            def att_copy_gram(t):
                act.wait_ge(s_G, t + 1)
                nc.scalar.copy(mat_a, misc[:, 0:D + 1]).then_inc(s_Gc, 1)

            def att_copy_mix(t):
                act.wait_ge(s_M, t + 1)
                nc.scalar.copy(mat_b, misc[:, 0:D]).then_inc(s_Mc, 1)

            def att_copy_fold(t):
                act.wait_ge(s_obias, t + 1)
                nc.scalar.copy(mat_a[:, 0:D], misc[:, 0:D]).then_inc(s_Pc, 1)

            def att_exp(t):
                act.wait_ge(s_smax, t + 1)
                nc.scalar.activation(mat_a[:, 0:D], misc[:, 0:D], ACT.Exp, bias=sm[:, 1:2], scale=SCALE,
                                     accum_out=sm[:, 2:3]).then_inc(s_exp, 1)

            def ffn_silu(t1):
                act.wait_ge(s_down, t1 * NB)
                nc.scalar.activation(yT, ffn_ps, ACT.Silu).then_inc(s_y, 1)

            def load_again(t):
                act.dma_start(x_again, x_v[bass.ds(t, 1)].rearrange("b p j d -> (b p) j d")).then_inc(s_xagain, 16)

            def store(t):
                act.wait_ge(s_res, t + 1)
                act.dma_start(out_v[bass.ds(t, 1)].rearrange("b p j d -> (b p) j d"), o_sb).then_inc(s_out, 16)

            def attention(t, n, n0):
                if n == n0 + 1:
                    att_copy_gram(t)
                if n == n0 + 6:
                    att_exp(t)
                if n == n0 + 10:
                    att_copy_mix(t)
                if n == n0 + 12:
                    att_copy_fold(t)

            act.dma_start(rt_raw[:, :], routerT).then_inc(s_rtc, 16)
            act.dma_start(col_sb[:, :], columns).then_inc(s_const, 16)
            act.dma_start(row_sb[:, :], rows.broadcast_to([P, rows.shape[1]])).then_inc(s_const, 16)
            nc.scalar.preload_act_table(ACT.Exp)
            split_hi(0)
            round_x(0)
            split_hi(1)
            split_hi(2)
            router_exp(True)
            nc.scalar.preload_act_table(ACT.Silu)
            copy_denseT(True)
            silu(0, 0, True)
            silu(0, 1, True)
            copy_pattern()
            split_hi(3)
            for n in range(NB):
                if n > 1:
                    silu(0, n, True)
                if n >= ROUND_LAG:
                    round_h(0, n - ROUND_LAG, True)
                c = chunk_at(n)
                if c >= 0:
                    split_hi(c)
                if n - 1 in XPOSE_AT:
                    round_x(XPOSE_AT[n - 1])
                if n == EXP:
                    router_exp(False)
                if n == OUT_T:
                    copy_denseT(False)
                    store_dense(act, False)
                if n == ATT0:
                    act.wait_ge(s_dram, 32)
                attention(0, n, ATT0)
            wait_split(act, NCHUNK - 1)
            wait_split(act, NCHUNK - 2)
            wait_split(act, NCHUNK - 3)
            load_again(0)
            with act.Fori(1, B) as t:
                for n in range(NB):
                    if n == LAG:
                        ffn_silu(t)
                    silu(t, n, False)
                    if n < ROUND_LAG:
                        round_h(t - 1, NB + n - ROUND_LAG, False)
                    else:
                        round_h(t, n - ROUND_LAG, False)
                    attention(t, n, ATT)
                    if n == LAG + 4:
                        store(t - 1)
                    if n == LAG + 9:
                        act.wait_ge(s_out, 16 * t)
                        load_again(t)
            for m in range(NB - ROUND_LAG, NB):
                round_h(B - 1, m, False)
            act.wait_ge(s_down, B * NB)
            for k in range(2):
                nc.scalar.activation(yT[:, half(k)], ffn_ps[:, half(k)], ACT.Silu).then_inc(s_y, 1)
            for k in range(2):
                act.wait_ge(s_res, B + k)
                j = slice(k * CH // 2, (k + 1) * CH // 2)
                act.dma_start(out_v[B - 1][:, j, :], o_sb[:, j, :]).then_inc(s_out, 16)
            act.wait_ge(s_out, 16 * (B + 1))

        @block.gpsimd
        def _(pool):
            count = [0]

            def step(ins):
                count[0] += 1
                ins.then_inc(s_pool, 1)
                pool.wait_ge(s_pool, count[0])

            def weigh(t, n, first):
                q = pattern_of[n]
                if n == 0 or pattern_of[n - 1] != q:
                    all_loads = loads(len(patterns) - SLOTS + q % SLOTS)
                    pool.wait_ge(s_route[q % SLOTS], t * all_loads + loads(q))
                pool.wait_ge(s_silu, t * NB + n + 1)
                s = s_buf[:, n % S_RING, :]
                nc.gpsimd.tensor_tensor(s, s, route[:, q % SLOTS, :], ALU.mult).then_inc(s_weighted, 1)

            def inverse_root(b):
                c = slice(b * CH, (b + 1) * CH)
                pool.wait_ge(s_var, b + 1)
                nc.gpsimd.tensor_tensor(rstd[:, c], ve[:, c], mhalf[:, c], ALU.pow).then_inc(s_rstd, 1)

            def second_root(b):
                c = slice(b * CH, (b + 1) * CH)
                pool.wait_ge(s_rstd, b + 1)
                step(nc.gpsimd.tensor_tensor(r2[:, c], mv[:, c, 1], rstd[:, c], ALU.mult))
                step(nc.gpsimd.tensor_tensor(r2[:, c], r2[:, c], rstd[:, c], ALU.mult))
                step(nc.gpsimd.tensor_scalar(r2[:, c], r2[:, c], LN_EPS, None, ALU.add))
                nc.gpsimd.tensor_tensor(r2[:, c], r2[:, c], mhalf[:, c], ALU.pow).then_inc(s_r2, 1)

            step(nc.gpsimd.memset(ident[:, :], 0.0))
            nc.gpsimd.affine_select(out=ident[:, :], in_=ident[:, :], compare_op=ALU.not_equal, fill=1.0, base=0,
                                    pattern=[[-1, P]], channel_multiplier=1).then_inc(s_ident, 1)
            step(nc.gpsimd.memset(mhalf[:, :], -0.5))
            inverse_root(0)
            inverse_root(1)
            split_lo(pool, 1)
            pool.wait_ge(s_const, 16 * N_CONST)
            nc.gpsimd.tensor_tensor(wv_n, wv_n, nw_bc, ALU.mult).then_inc(s_attw, 1)
            for n in range(NB):
                c = chunk_at(n)
                weigh(0, n, True)
                if c >= 0 and by_pool(c):
                    split_lo(pool, c)
                if n in ROOT_AT:
                    inverse_root(ROOT_AT[n])
                if n in ROOT2_AT:
                    second_root(ROOT2_AT[n])
            with pool.Fori(1, B) as t:
                for n in range(NB):
                    weigh(t, n, False)

        @block.vector
        def _(dve):
            count = [0]

            def step(ins):
                count[0] += 1
                ins.then_inc(s_dve, 1)
                dve.wait_ge(s_dve, count[0])

            def ln_stats(b):
                dve.wait_ge(s_x[b], 16)
                for j in range(CH):
                    last = nc.vector.bn_stats(stats[:, j, :], xn[:, b * CH + j, :])
                step(last)
                for j in range(CH):
                    last = nc.vector.bn_aggr(mv[:, b * CH + j, :], stats[:, j, :])
                step(last)
                c = slice(b * CH, (b + 1) * CH)
                nc.vector.tensor_scalar(ve[:, c], mv[:, c, 1], LN_EPS, None, ALU.add).then_inc(s_var, 1)

            def ln_apply(b):
                dve.wait_ge(s_rstd, b + 1)
                for j in range(b * CH, (b + 1) * CH):
                    last = nc.vector.tensor_scalar(xn[:, j, :], xn[:, j, :], mv[:, j, 0:1], rstd[:, j:j + 1],
                                                   ALU.subtract, ALU.mult)
                last.then_inc(s_ln, 1)

            def split_x(b):
                dve.wait_ge(s_xhi, b + 1)
                c = slice(b * L, (b + 1) * L)
                nc.vector.tensor_tensor(xT_lo[:, c], misc, xT_hi[:, c].bitcast(F32), ALU.subtract).then_inc(s_xlo, 1)

            def sum_logits(b):
                k = max(b - 1, 0) * CH
                dve.wait_ge(s_logit, b + 1)
                parts = misc[:, 0:2 * CH * E].rearrange("p (j h e) -> p j h e", h=2, e=E)
                nc.vector.tensor_copy(lg[:, k:k + CH, :], parts[:, :, 0, :]).then_inc(s_lsum, 1)
                dve.wait_ge(s_lsum, b + 1)
                nc.vector.tensor_tensor(lg[:, k:k + CH, :], parts[:, :, 1, :], lg[:, k:k + CH, :],
                                        ALU.add).then_inc(s_logits, 1)

            def pick_top(k0, k):
                for j in range(k0, k0 + k):
                    last = nc.vector.max(top8[:, j, :], lg[:, j, :])
                step(last)
                for j in range(k0, k0 + k):
                    last = nc.vector.match_replace(lr[:, j, :], top8[:, j, :], lg[:, j, :], NEG)
                step(last)

            def shift_logits(k):
                nc.vector.tensor_tensor(ex[:, 0:k, :], lg[:, 0:k, :], top8[:, 0:k, 0:1].broadcast_to([P, k, E]),
                                        ALU.subtract).then_inc(s_lmax, 1)

            def mark_chosen(k):
                step(nc.vector.tensor_tensor(lr[:, 0:k, :], lr[:, 0:k, :], lg[:, 0:k, :], ALU.not_equal))

            def sum_chosen(first):
                k = CH if first else NR
                dve.wait_ge(s_lexp, 1 if first else 2)
                step(nc.vector.tensor_tensor(ex[:, 0:k, :], ex[:, 0:k, :], lr[:, 0:k, :], ALU.mult))
                step(nc.vector.tensor_reduce(rsum[:, 0:k], ex[:, 0:k, :], AX_X, ALU.add))
                step(nc.vector.reciprocal(rsum[:, NR:NR + k], rsum[:, 0:k]))

            def dense_weights(first):
                k = CH if first else NR
                for b in range(k // CH):
                    j = slice(b * CH, (b + 1) * CH)
                    last = nc.vector.tensor_tensor(
                        dense[:, b, :, :].rearrange("p e j -> p j e"), ex[:, j, :],
                        rsum[:, NR + b * CH:NR + (b + 1) * CH].unsqueeze(2).broadcast_to([P, CH, E]), ALU.mult)
                last.then_inc(s_dense, 1)

            def hidden(t, n):
                dve.wait_ge(s_up, t * NB + n + 1)
                dve.wait_ge(s_weighted, t * NB + n + 1)
                nc.vector.tensor_tensor(up_ps[n % U_RING], s_buf[:, n % S_RING, :], up_ps[n % U_RING],
                                        ALU.mult).then_inc(s_h, 1)

            def split_h(t, m):
                dve.wait_ge(s_hhi, t * NB + m + 1)
                nc.vector.tensor_tensor(h_lo[:, m % H_RING, :], up_ps[m % U_RING], h_hi[:, m % H_RING, :].bitcast(F32),
                                        ALU.subtract).then_inc(s_hlo, 1)

            def spread_norm_b():
                dve.wait_ge(s_const, 16 * N_CONST)
                step(nc.vector.memset(nb_bc[:, :], 1.0))
                nc.vector.tensor_scalar(nb_bc[:, :], nb_bc[:, :], nb_col, None, ALU.mult).then_inc(s_nb, 1)

            def fold_norm():
                dve.wait_ge(s_bias, 1)
                nc.vector.tensor_scalar(wqkT, wqkT, nw_col, None, ALU.mult).then_inc(s_attw, 1)
                step(nc.vector.tensor_tensor(bkL_row[:, :], bias_ps[0:1, D:2 * D], bk_bc[0:1, :], ALU.add))
                step(nc.vector.tensor_scalar(bkL_row[:, :], bkL_row[:, :], float(L), None, ALU.mult))
                nc.vector.tensor_tensor(bq_row, bias_ps[0:1, 0:D], bq_row, ALU.add).then_inc(s_attw, 1)
                nc.vector.tensor_tensor(bk_bc, bias_ps[:, 2 * D:3 * D], bk_bc, ALU.add).then_inc(s_attw, 1)
                nc.vector.tensor_scalar(bv_bc[:, :], bias_ps[:, 3 * D:4 * D], bv_col, None, ALU.add).then_inc(s_attw, 1)

            def att_copy_keys(t):
                dve.wait_ge(s_X, t + 1)
                nc.vector.scalar_tensor_tensor(out=mat_b, in0=bk_bc, scalar=mat_a[:, D:D + 1],
                                               in1=misc[:, 0:D], op0=ALU.mult, op1=ALU.add).then_inc(s_Xc, 1)
                nc.vector.tensor_tensor(r_row[:, :], misc[0:1, D:2 * D], bkL_row[:, :], ALU.add).then_inc(s_Xc, 1)

            def att_max(t, t2):
                dve.wait_ge(s_S, t + 1)
                nc.vector.tensor_reduce(sm[:, 0:1], misc[:, 0:D], AX_X, ALU.max).then_inc(s_dve, 1)
                dve.wait_ge(s_dve, t2 + 2)
                nc.vector.tensor_scalar(sm[:, 1:2], sm[:, 0:1], -SCALE, None, ALU.mult).then_inc(s_smax, 1)

            def att_normalise(t, t2):
                dve.wait_ge(s_exp, t + 1)
                nc.vector.reciprocal(sm[:, 3:4], sm[:, 2:3]).then_inc(s_dve, 1)
                dve.wait_ge(s_dve, t2 + 3)
                nc.vector.tensor_scalar(mat_a[:, 0:D], mat_a[:, 0:D], sm[:, 3:4], None, ALU.mult).then_inc(s_w, 1)

            def att_bias(t):
                dve.wait_ge(s_P, t + 1)
                nc.vector.tensor_tensor(out_bias, misc[:, D:2 * D], pb_bc, ALU.add).then_inc(s_obias, 1)
                v = xn[:, bass.ds(t * CH, CH), :]
                dve.wait_ge(s_obias, t + 1)
                nc.vector.tensor_tensor(v, v, out_bias.unsqueeze(1).broadcast_to([P, CH, D]),
                                        ALU.add).then_inc(s_biased, 1)

            def att_finish(t):
                dve.wait_ge(s_U, t + 1)
                dve.wait_ge(s_biased, t + 1)
                for j in range(CH):
                    v = xn[:, bass.ds(t * CH + j, 1), :].rearrange("p o d -> p (o d)")
                    last = nc.vector.scalar_tensor_tensor(out=v, in0=misc[:, j * D:(j + 1) * D],
                                                          scalar=r2_cur[:, j:j + 1], in1=v, op0=ALU.mult, op1=ALU.add)
                last.then_inc(s_attn, 1)

            def make_z(t, t2):
                nc.vector.tensor_copy(r2_cur[:, :], r2[:, bass.ds(t * CH, CH)]).then_inc(s_dve, 1)
                nc.vector.memset(z[:, :, D:D + 1], 1.0).then_inc(s_z, 1)
                dve.wait_ge(s_dve, t2 + 1)
                nc.vector.tensor_tensor(z[:, :, 0:D], xn[:, bass.ds(t * CH, CH), :],
                                        r2_cur[:, :].unsqueeze(2).broadcast_to([P, CH, D]), ALU.mult).then_inc(s_z, 1)

            def make_x_cur(t):
                nc.vector.tensor_tensor(x_cur, tile_cols(xT_hi, t).bitcast(F32), tile_cols(xT_lo, t).bitcast(F32),
                                        ALU.add).then_inc(s_xcur, 1)

            def attention(t, t3, n, n0):
                if n == n0 - 3:
                    make_z(t, t3)
                if n == n0 + 1:
                    dve.wait_ge(s_G, t + 1)
                    make_x_cur(t)
                if n == n0 + 2:
                    att_copy_keys(t)
                if n == n0 + 4:
                    att_max(t, t3)
                if n == n0 + 7:
                    att_normalise(t, t3)
                if n == n0 + 11:
                    att_bias(t)
                if n == n0 + 13:
                    att_finish(t)

            def combine(t):
                dve.wait_ge(s_yT, t + 1)
                dve.wait_ge(s_xagain, 16 * t + 16)
                nc.vector.tensor_tensor(o_sb, misc.rearrange("p (j d) -> p j d", j=CH),
                                        xn[:, bass.ds(t * CH, CH), :], ALU.mult).then_inc(s_comb, 1)
                dve.wait_ge(s_comb, t + 1)
                nc.vector.tensor_tensor(o_sb, o_sb, x_again, ALU.add).then_inc(s_res, 1)

            ln_stats(0)
            dve.wait_ge(s_rtc, 16)
            nc.vector.tensor_copy(rt_hi, rt_raw[:, :]).then_inc(s_rt, 1)
            dve.wait_ge(s_rt, 1)
            nc.vector.tensor_tensor(rt_lo, rt_raw[:, :], rt_hi.bitcast(F32),
                                    ALU.subtract).then_inc(s_rt, 1)
            ln_apply(0)
            split_lo(dve, 0)
            spread_norm_b()
            split_x(0)
            ln_stats(1)
            sum_logits(0)
            dve.wait_ge(s_logits, 1)
            pick_top(0, CH)
            shift_logits(CH)
            mark_chosen(CH)
            sum_chosen(True)
            dense_weights(True)
            fold_norm()
            ln_apply(1)
            split_lo(dve, 2)
            ln_stats(2)
            for n in range(NB):
                c = chunk_at(n)
                if n >= ROUND_LAG:
                    split_h(0, n - ROUND_LAG)
                if n == 3:
                    split_lo(dve, AHEAD - 1)
                if c >= 0 and not by_pool(c):
                    split_lo(dve, c)
                if n - 1 in XPOSE_AT:
                    split_x(XPOSE_AT[n - 1])
                if n in STATS_AT:
                    ln_stats(STATS_AT[n])
                if n in APPLY_AT:
                    ln_apply(APPLY_AT[n])
                if n in ROUTER_AT:
                    sum_logits(ROUTER_AT[n])
                if n in PICK_AT:
                    dve.wait_ge(s_logits, PICK_AT[n] + 1)
                    pick_top((PICK_AT[n] - 1) * CH, CH)
                if n == SHIFT:
                    dve.wait_ge(s_dram, 16)
                    shift_logits(NR)
                if n == MARK:
                    mark_chosen(NR)
                if n == SUM:
                    sum_chosen(False)
                if n == WEIGHTS:
                    dense_weights(False)
                if n == ATT0 - 3:
                    dve.wait_ge(s_r2, B)
                    dve.wait_ge(s_dense, 2)
                attention(0, count[0], n, ATT0)
                hidden(0, n)
            base = count[0]
            with dve.Fori(1, B) as t:
                for n in range(NB):
                    if n < ROUND_LAG:
                        split_h(t - 1, NB + n - ROUND_LAG)
                    else:
                        split_h(t, n - ROUND_LAG)
                    if n == LAG + 1:
                        combine(t - 1)
                    attention(t, t * 3 + base, n, ATT)
                    hidden(t, n)
            for m in range(NB - ROUND_LAG, NB):
                split_h(B - 1, m)
            dve.wait_ge(s_xagain, 16 * B)
            for k in range(2):
                dve.wait_ge(s_yT, B + k)
                j = slice(k * CH // 2, (k + 1) * CH // 2)
                nc.vector.tensor_tensor(o_sb[:, j, :], end_ps[k][:, 0:L // 2].rearrange("p (j d) -> p j d", d=D),
                                        xn[:, (B - 1) * CH:B * CH, :][:, j, :], ALU.mult).then_inc(s_comb, 1)
                dve.wait_ge(s_comb, B + k)
                nc.vector.tensor_tensor(o_sb[:, j, :], o_sb[:, j, :], x_again[:, j, :], ALU.add).then_inc(s_res, 1)


def kernel(L0_attn_x, L0_attn_norm_w, L0_attn_norm_b, L0_attn_qkv_w, L0_attn_qkv_b, L0_attn_proj_w, L0_attn_proj_b,
           L0_ffn_router_w, L0_ffn_gate_w, L0_ffn_up_w, L0_ffn_down_w):
    import numpy as np
    import concourse.bacc as bacc
    from concourse.bass_utils import run_bass_kernel_spmd

    x = np.asarray(L0_attn_x)
    B, L, D = x.shape
    qkv_w = np.asarray(L0_attn_qkv_w)
    E, F, H = L0_ffn_gate_w.shape
    NB = E * F // P
    gate = np.asarray(L0_ffn_gate_w).reshape(NB, P, H).transpose(2, 0, 1)
    up = np.asarray(L0_ffn_up_w).reshape(NB, P, H).transpose(2, 0, 1)
    down = np.asarray(L0_ffn_down_w).transpose(0, 2, 1).reshape(NB, P, H).transpose(1, 0, 2)
    norm_w, norm_b, qkv_b, proj_b = (np.asarray(v) for v in (L0_attn_norm_w, L0_attn_norm_b, L0_attn_qkv_b,
                                                             L0_attn_proj_b))
    arrays = {
        "x": x,
        "columns": np.concatenate([qkv_w.T, qkv_w[2 * D:], np.asarray(L0_attn_proj_w).T, norm_w[:, None],
                                   norm_b[:, None], qkv_b[2 * D:, None]], axis=1),
        "rows": np.concatenate([norm_w, qkv_b, proj_b])[None, :],
        "routerT": np.asarray(L0_ffn_router_w).T, "w_all": np.stack([gate, up, down], axis=2),
    }
    arrays = {k: np.ascontiguousarray(v) for k, v in arrays.items()}
    nc = bacc.Bacc("TRN2", target_bir_lowering=False, num_devices=1)
    args = [nc.dram_tensor(k, v.shape, F32, kind="ExternalInput").ap() for k, v in arrays.items()]
    dense = nc.dram_tensor("dense_w", (B * E, L), F32, kind="Internal").ap()
    out = nc.dram_tensor("out", (B, L, D), F32, kind="ExternalOutput").ap()
    gated_block(nc, *args, dense, out)
    r = run_bass_kernel_spmd(nc, [arrays], core_ids=[0])
    return r.results[0]["out"]
```
